# Optimizing a Trainium2 kernel written in Bass

```python
import numpy as np
import jax
import jax.numpy as jnp

def _softmax(x, axis=-1):
    return jax.nn.softmax(x, axis=axis)

def _gelu(x):
    return jax.nn.gelu(x, approximate=True)

def _silu(x):
    return jax.nn.silu(x)

def _sigmoid(x):
    return jax.nn.sigmoid(x)

def _layernorm(x, axis=-1, eps=1e-05):
    m = jnp.mean(x, axis=axis, keepdims=True)
    v = jnp.var(x, axis=axis, keepdims=True)
    return (x - m) / jnp.sqrt(v + eps)

def _scatter_add(tgt, idx, src, axis=0):
    return tgt.at[idx].add(src)

def _segment_sum(src, seg, n):
    return jax.ops.segment_sum(src, seg, n)
kernel_name = 'mk_seq_preln_d2_jaxref_r8_41b360'

def setup_inputs(seed: int=0):
    np.random.seed(seed)
    _w = jnp.asarray

    def _L0_attn_setup():
        import jax, jax.numpy as jnp
        import numpy as np
        EPS = 1e-06
        NUM_HEADS = 16

        def rms_norm(x, w):
            var = jnp.mean(jnp.square(x), axis=-1, keepdims=True)
            return x * jax.lax.rsqrt(var + EPS) * w
        key = jax.random.key(seed)
        ks = jax.random.split(key, 6)
        B, N, C = (8, 128, 128)
        return {'x': jax.random.normal(ks[0], (B, N, C), dtype=jnp.float32), 'w_qkv': jax.random.normal(ks[1], (3 * C, C), dtype=jnp.float32) * (1.0 / np.sqrt(C)), 'b_qkv': jax.random.normal(ks[2], (3 * C,), dtype=jnp.float32) * 0.02, 'qn_w': jnp.ones((C // NUM_HEADS,), dtype=jnp.float32), 'kn_w': jnp.ones((C // NUM_HEADS,), dtype=jnp.float32), 'w_proj': jax.random.normal(ks[3], (C, C), dtype=jnp.float32) * (1.0 / np.sqrt(C)), 'b_proj': jax.random.normal(ks[4], (C,), dtype=jnp.float32) * 0.02}
    _L0_attn_in = _L0_attn_setup()

    def _L0_ffn_setup():
        import jax, jax.numpy as jnp
        import numpy as np
        TOP_K = 2
        E = 8
        D = 128
        F = 256
        B, S = (2, 128)
        key = jax.random.key(seed)
        ks = jax.random.split(key, 8)
        sc = 0.02
        return {'x_bsD': jax.random.normal(ks[0], (B, S, D), dtype=jnp.float32), 'router_DE': jax.random.normal(ks[1], (D, E), dtype=jnp.float32) * sc, 'w_in_shared_FD': jax.random.normal(ks[2], (F, D), dtype=jnp.float32) * sc, 'w_out_shared_DF': jax.random.normal(ks[3], (D, F), dtype=jnp.float32) * sc, 'w_swiglu_FD': jax.random.normal(ks[4], (F, D), dtype=jnp.float32) * sc, 'w_in_eDF': jax.random.normal(ks[5], (E, D, F), dtype=jnp.float32) * sc, 'w_swiglu_eDF': jax.random.normal(ks[6], (E, D, F), dtype=jnp.float32) * sc, 'w_out_eFD': jax.random.normal(ks[7], (E, F, D), dtype=jnp.float32) * sc}
    _L0_ffn_in = _L0_ffn_setup()

    def _L1_attn_setup():
        import jax, jax.numpy as jnp
        import numpy as np
        B, T = (2, 256)
        TOK, POS = (64, 64)
        H, D, KVH = (16, 64, 4)
        key = jax.random.key(seed)
        ks = jax.random.split(key, 7)

        def w(k, shape, fan_in):
            return jax.random.normal(k, shape, jnp.float32) / np.float32(np.sqrt(fan_in))
        x = jax.random.normal(ks[0], (B, T, TOK + POS), jnp.float32)
        Wq = w(ks[1], (POS, H * D), POS)
        Wk = w(ks[2], (POS, KVH * D), POS)
        Wv = w(ks[3], (TOK, KVH * D), TOK)
        Wo = w(ks[4], (H * D, TOK + POS), H * D)
        q_phase_angle = 0.1 * jax.random.normal(ks[5], (H,), jnp.float32)
        alibi_log_slopes = jnp.full((H,), np.float32(np.log(np.log(10.0))))
        return dict(x=x, Wq=Wq, Wk=Wk, Wv=Wv, Wo=Wo, q_phase_angle=q_phase_angle, alibi_log_slopes=alibi_log_slopes)
    _L1_attn_in = _L1_attn_setup()

    def _L1_ffn_setup():
        import jax, jax.numpy as jnp
        import numpy as np
        key = jax.random.key(seed)
        kx, kw = jax.random.split(key)
        x = jax.random.normal(kx, (32, 512, 128), dtype=jnp.float32)
        weight = jax.random.normal(kw, (128, 128), dtype=jnp.float32) * 0.01
        return {'x': x, 'weight': weight}
    _L1_ffn_in = _L1_ffn_setup()
    _d = {'L0_attn_x': _L0_attn_in['x'], 'L0_attn_w_qkv': _L0_attn_in['w_qkv'], 'L0_attn_b_qkv': _L0_attn_in['b_qkv'], 'L0_attn_qn_w': _L0_attn_in['qn_w'], 'L0_attn_kn_w': _L0_attn_in['kn_w'], 'L0_attn_w_proj': _L0_attn_in['w_proj'], 'L0_attn_b_proj': _L0_attn_in['b_proj'], 'L0_ffn_router_DE': _L0_ffn_in['router_DE'], 'L0_ffn_w_in_shared_FD': _L0_ffn_in['w_in_shared_FD'], 'L0_ffn_w_out_shared_DF': _L0_ffn_in['w_out_shared_DF'], 'L0_ffn_w_swiglu_FD': _L0_ffn_in['w_swiglu_FD'], 'L0_ffn_w_in_eDF': _L0_ffn_in['w_in_eDF'], 'L0_ffn_w_swiglu_eDF': _L0_ffn_in['w_swiglu_eDF'], 'L0_ffn_w_out_eFD': _L0_ffn_in['w_out_eFD'], 'L1_attn_Wq': _L1_attn_in['Wq'], 'L1_attn_Wk': _L1_attn_in['Wk'], 'L1_attn_Wv': _L1_attn_in['Wv'], 'L1_attn_Wo': _L1_attn_in['Wo'], 'L1_attn_q_phase_angle': _L1_attn_in['q_phase_angle'], 'L1_attn_alibi_log_slopes': _L1_attn_in['alibi_log_slopes'], 'L1_ffn_weight': _L1_ffn_in['weight']}
    _x0 = _d['L0_attn_x']
    _d['L0_attn_x'] = jax.random.normal(jax.random.fold_in(jax.random.key(seed), 1), (16, 512, 128), dtype=_x0.dtype)
    del _x0
    return _d

def reference(L0_attn_x, L0_attn_w_qkv, L0_attn_b_qkv, L0_attn_qn_w, L0_attn_kn_w, L0_attn_w_proj, L0_attn_b_proj, L0_ffn_router_DE, L0_ffn_w_in_shared_FD, L0_ffn_w_out_shared_DF, L0_ffn_w_swiglu_FD, L0_ffn_w_in_eDF, L0_ffn_w_swiglu_eDF, L0_ffn_w_out_eFD, L1_attn_Wq, L1_attn_Wk, L1_attn_Wv, L1_attn_Wo, L1_attn_q_phase_angle, L1_attn_alibi_log_slopes, L1_ffn_weight):

    def _L0_attn_ref(x, w_qkv, b_qkv, qn_w, kn_w, w_proj, b_proj):
        import jax, jax.numpy as jnp
        import numpy as np
        EPS = 1e-06
        NUM_HEADS = 16

        def rms_norm(x, w):
            var = jnp.mean(jnp.square(x), axis=-1, keepdims=True)
            return x * jax.lax.rsqrt(var + EPS) * w
        B, N, C = x.shape
        H = NUM_HEADS
        D = C // H
        qkv = x @ w_qkv.T + b_qkv
        qkv = qkv.reshape(B, N, 3, H, D).transpose(2, 0, 3, 1, 4)
        q, k, v = (qkv[0], qkv[1], qkv[2])
        q = rms_norm(q, qn_w)
        k = rms_norm(k, kn_w)
        scale = 1.0 / np.sqrt(D).astype(np.float32)
        attn = jnp.einsum('bhld,bhsd->bhls', q, k) * scale
        attn = jax.nn.softmax(attn, axis=-1)
        out = jnp.einsum('bhls,bhsd->bhld', attn, v)
        out = out.transpose(0, 2, 1, 3).reshape(B, N, C)
        return out @ w_proj.T + b_proj

    def _L0_ffn_ref(x_bsD, router_DE, w_in_shared_FD, w_out_shared_DF, w_swiglu_FD, w_in_eDF, w_swiglu_eDF, w_out_eFD):
        import jax, jax.numpy as jnp
        import numpy as np
        TOP_K = 2
        E = 8
        D = 128
        F = 256
        B, S = (2, 128)
        b, s, d = x_bsD.shape
        x_aD = x_bsD.reshape(-1, d)
        a = x_aD.shape[0]
        scores_aE = x_aD @ router_DE
        topv_aK, topi_aK = jax.lax.top_k(scores_aE, TOP_K)
        masked_aE = jnp.full_like(scores_aE, -jnp.inf)
        masked_aE = masked_aE.at[jnp.arange(a)[:, None], topi_aK].set(topv_aK)
        gates_Ea = jax.nn.sigmoid(masked_aE.astype(jnp.float32)).astype(x_aD.dtype).T
        routed_in_EaD = x_aD[None, :, :] * gates_Ea[:, :, None]
        routed_in_EaD = jax.lax.stop_gradient(routed_in_EaD)
        mid_EaF = jnp.einsum('ead,edf->eaf', routed_in_EaD, w_in_eDF)
        sw_EaF = jnp.einsum('ead,edf->eaf', routed_in_EaD, w_swiglu_eDF)
        h_EaF = jax.nn.silu(mid_EaF) * sw_EaF
        out_EaD = jnp.einsum('eaf,efd->ead', h_EaF, w_out_eFD)
        shared_aF = jax.nn.silu(x_aD @ w_in_shared_FD.T) * (x_aD @ w_swiglu_FD.T)
        shared_out_aD = jax.lax.stop_gradient(shared_aF @ w_out_shared_DF.T)
        out_aD = shared_out_aD + jnp.sum(out_EaD, axis=0)
        return out_aD.reshape(b, s, d)

    def _L1_attn_ref(x, Wq, Wk, Wv, Wo, q_phase_angle, alibi_log_slopes):
        import jax, jax.numpy as jnp
        import numpy as np
        B, T = (2, 256)
        TOK, POS = (64, 64)
        H, D, KVH = (16, 64, 4)
        b, t, _ = x.shape
        x_tok = x[:, :, :TOK]
        x_pos = x[:, :, TOK:]
        q = (x_pos @ Wq).reshape(b, t, H, D).transpose(0, 2, 1, 3)
        k = (x_pos @ Wk).reshape(b, t, KVH, D).transpose(0, 2, 1, 3)
        v = (x_tok @ Wv).reshape(b, t, KVH, D).transpose(0, 2, 1, 3)
        c = jnp.cos(q_phase_angle)[None, :, None, None]
        s = jnp.sin(q_phase_angle)[None, :, None, None]
        q2 = q.reshape(b, H, t, D // 2, 2)
        q0, q1 = (q2[..., 0], q2[..., 1])
        q = jnp.stack([q0 * c - q1 * s, q0 * s + q1 * c], axis=-1).reshape(b, H, t, D)
        rep = H // KVH
        k = jnp.repeat(k, rep, axis=1)
        v = jnp.repeat(v, rep, axis=1)
        att = jnp.einsum('bhqd,bhkd->bhqk', q, k) / np.float32(np.sqrt(D))
        pos = jnp.arange(t)
        rel = (pos[:, None] - pos[None, :]).astype(jnp.float32)
        att = att + jnp.exp(alibi_log_slopes)[None, :, None, None] * rel[None, None]
        mask = pos[:, None] >= pos[None, :]
        att = jnp.where(mask[None, None], att, -jnp.inf)
        m = jnp.max(att, axis=-1, keepdims=True)
        e = jnp.exp(att - m)
        att = e / (1.0 + jnp.sum(e, axis=-1, keepdims=True))
        out = jnp.einsum('bhqk,bhkd->bhqd', att, v)
        out = out.transpose(0, 2, 1, 3).reshape(b, t, H * D)
        return out @ Wo

    def _L1_ffn_ref(x, weight):
        import jax, jax.numpy as jnp
        import numpy as np
        b_weight = jnp.sign(weight)
        return jnp.einsum('bsi,oi->bso', x, b_weight)
    x = L0_attn_x
    x = x + _L0_attn_ref(_layernorm(x, axis=-1), L0_attn_w_qkv, L0_attn_b_qkv, L0_attn_qn_w, L0_attn_kn_w, L0_attn_w_proj, L0_attn_b_proj)
    x = x + _L0_ffn_ref(_layernorm(x, axis=-1), L0_ffn_router_DE, L0_ffn_w_in_shared_FD, L0_ffn_w_out_shared_DF, L0_ffn_w_swiglu_FD, L0_ffn_w_in_eDF, L0_ffn_w_swiglu_eDF, L0_ffn_w_out_eFD)
    x = x + _L1_attn_ref(_layernorm(x, axis=-1), L1_attn_Wq, L1_attn_Wk, L1_attn_Wv, L1_attn_Wo, L1_attn_q_phase_angle, L1_attn_alibi_log_slopes)
    x = x + _L1_ffn_ref(_layernorm(x, axis=-1), L1_ffn_weight)
    return x

_drawn_inputs = setup_inputs


def setup_inputs(seed=0):
    import zlib

    import numpy as np

    out = dict(_drawn_inputs(seed))
    spreads = {'L0_attn_qn_w': (1.0, 0.6),
     'L0_attn_kn_w': (1.0, 0.6),
     'L1_attn_alibi_log_slopes': (0.834032416343689, 0.6)}
    factors = {'L0_attn_b_proj': 3.231,
     'L0_ffn_router_DE': 8.0,
     'L0_ffn_w_in_shared_FD': 6.459,
     'L0_ffn_w_out_shared_DF': 6.484,
     'L0_ffn_w_swiglu_FD': 6.498,
     'L0_ffn_w_in_eDF': 8.0,
     'L0_ffn_w_swiglu_eDF': 8.0,
     'L0_ffn_w_out_eFD': 8.0,
     'L1_attn_q_phase_angle': 34.224,
     'L1_attn_Wq': 2.964,
     'L1_attn_Wk': 2.906}
    for name, (base, spread) in spreads.items():
        noise = np.random.default_rng([zlib.crc32(name.encode()), seed]).standard_normal(out[name].shape)
        drawn = base * np.exp(spread * noise) if base else spread * noise
        out[name] = jnp.asarray(drawn.astype(out[name].dtype))
    for name, factor in factors.items():
        out[name] = (out[name] * factor).astype(out[name].dtype)
    return out
```

```python
from contextlib import ExitStack
import math

import concourse.bass as bass
from concourse import mybir

F32 = mybir.dt.float32
F32R = mybir.dt.float32r
I32 = mybir.dt.int32
U32 = mybir.dt.uint32
ALU = mybir.AluOpType
ACT = mybir.ActivationFunctionType
AX = mybir.AxisListType

P = 128
C = 128
T = 512
NT = T // P

H0, D0 = 16, 8
G0 = 4
NG = H0 // G0
ROWS = P // G0
AUG = 3 * D0
QK = 2 * C
VW = D0 + 1
LEAD = 5

E, F = 8, 256
NE = E + 1
FT = F // P

H1, D1, KVH = 16, 64, 4
REP = H1 // KVH
CAUSAL = P * NT * (NT + 1) // 2
ROW_AT = [P * i * (i + 1) // 2 for i in range(NT)]
KEY_AT = [0, 512, 1024, 896]
TURN = (6.28125, 2 * math.pi - 6.28125)
PI_DOWN = 3.1415925
LN_EPS, RMS_EPS = 1e-5, 1e-6
BIG = 3.0e38

PARTS = [("qkv", 3 * C), ("proj", C), ("win", NE * F), ("wsw", NE * F), ("wout", NE * F), ("wq", H1 * D1),
         ("wk", 2 * KVH * D1), ("wv", KVH * D1), ("wo", H1 * D1 // P * C), ("sign", C)]
COL = {}
NW = 0
for _name, _n in PARTS:
    COL[_name] = NW
    NW += _n


def kernel_program(nc, x, w_all, b_qkv, b_proj, qn_w, kn_w, router, angle, slopes, out):
    NB = x.shape[0]
    x_dram = x.rearrange("b (t p) c -> b p t c", p=P)
    out_dram = out.rearrange("b (t p) c -> b p t c", p=P)

    with ExitStack() as ctx:
        def sb(name, shape, dt=F32):
            return ctx.enter_context(nc.sbuf_tensor(name, shape, dt))

        def sem(name):
            return ctx.enter_context(nc.semaphore(name))

        w_hi = sb("w_hi", [P, NW], F32R)
        w_lo = sb("w_lo", [P, NW], F32R)
        ident = sb("ident", [P, P])
        b_qkv_sb = sb("b_qkv_sb", [P, 3 * C])
        b_proj_sb = sb("b_proj_sb", [P, C])
        norm_w_raw = sb("norm_w_raw", [P, 2, D0])
        norm_w = sb("norm_w", [P, 2, H0, D0])
        router_sb = sb("router_sb", [P, E])
        x_in = sb("x_in", [P, NT, C])
        x_res = sb("x_res", [P, NT, C])
        v_nat = sb("v_nat", [P, NT, VW * H0 + ROWS - VW])
        expert_ids = sb("expert_ids", [P, E])
        pick = sb("pick", [2 * E, E], F32R)
        alibi = sb("alibi", [P, H1, T])
        angle_sb = sb("angle_sb", [P, 4, H1])
        slope_sb = sb("slope_sb", [P, H1])
        neg_m = sb("neg_m", [P, H1, NT])
        sums = sb("sums", [P, H1, NT])
        rden = sb("rden", [P, H1, NT])
        stats = sb("stats", [P, NT, 6])
        mean_var = sb("mean_var", [P, NT, 2])
        rstd = sb("rstd", [P, NT])
        newton = sb("newton", [P, NT])
        shared = sb("shared", [P, 11008])
        shared_r = sb("shared_r", [P, 10240], F32R)

        def carve(arena, at, *shape):
            n = math.prod(shape)
            ap = arena[:, at:at + n]
            names = "abcd"[:len(shape)]
            if len(shape) == 1:
                return ap
            return ap.rearrange(f"p ({' '.join(names)}) -> p {' '.join(names)}", **dict(zip(names, shape)))

        raw = shared[:, 0:NW]
        nat_q = carve(shared, 0, NT, H0, ROWS)
        nat_k = carve(shared, 2048, NT, H0, ROWS)
        probs = carve(shared, 4096, 2, G0, T)
        xn = carve(shared, 4096, NT, C)
        qkv = carve(shared, 4608, NT, 3 * C)
        qk_sq = carve(shared, 6144, NT, QK)
        qk_w = carve(shared, 8192, NT, QK)
        o_t = carve(shared, 9216, T)
        o_nat = carve(shared, 9728, NT, C)
        ms = carve(shared, 10240, NT, 2 * H0)
        ms_y = carve(shared, 10368, NT, 2 * H0)
        ms_t = carve(shared, 10496, NT, 2 * H0)
        neg_max = carve(shared, 10624, NT, H0)
        rec = carve(shared, 10688, NT, G0)
        x_t = carve(shared_r, 0, 2, T)
        q_z = carve(shared_r, 0, G0, T)
        k_t = carve(shared_r, 2048, NG, T)
        q_t = carve(shared_r, 4096, NG, T)
        k_z = carve(shared_r, 6144, 2, G0, T)
        a_t = carve(shared_r, 2048, 2, T)

        xn2 = carve(shared, 0, NT, C)
        x_tf = carve(shared, 512, T)
        x_gated = carve(shared, 1024, 2, T)
        silu = carve(shared, 2048, 2, FT, T)
        hidden = carve(shared, 4096, 2, FT, T)
        moe_t = carve(shared, 6144, T)
        scores_sb = carve(shared, 6656, NT, E)
        top = carve(shared, 6688, NT, E)
        top_at = carve(shared, 6720, NT, E)
        top_atf = carve(shared, 6752, NT, 2)
        chosen = carve(shared, 6784, 2, NT, E)
        gate_exp = carve(shared, 6848, NT, E)
        gate = carve(shared, 6880, NT, E)
        gates_nat = carve(shared, 6912, NT, 2 * E)
        xg_r = carve(shared_r, 0, 2, 2, T)
        h_r = carve(shared_r, 2048, 2, 2, FT, T)
        g_t = carve(shared_r, 6144, T)

        x_dup = carve(shared, 0, NT, 2, 2, D1)
        v1 = carve(shared, 1024, NT, KVH * D1)
        att = carve(shared, 2048, 3, CAUSAL)
        probs_t = carve(shared, 5888, 4, CAUSAL)
        wo_t = carve(shared, 0, T)
        xn4 = carve(shared, 512, NT, C)
        tok_r = carve(shared_r, 0, T)
        pos_r = carve(shared_r, 512, T)
        k_r = carve(shared_r, 1024, KVH, 2, T)
        q_r = carve(shared_r, 5120, 4, T)
        o_r = carve(shared_r, 7168, 1, 2, T)
        f_r = carve(shared_r, 0, 2, T)

        psum = ctx.enter_context(nc.psum_tensor("psum", [P, 8, T], F32))

        def bank(i):
            return psum[:, i, :]

        def whi(part, a, n):
            return w_hi[:, COL[part] + a:COL[part] + a + n]

        def wlo(part, a, n):
            return w_lo[:, COL[part] + a:COL[part] + a + n]

        weights_in = sem("weights_in")
        consts_in = sem("consts_in")
        ident_ready = sem("ident_ready")
        w_hi_ready = sem("w_hi_ready")
        w_lo_ready = sem("w_lo_ready")
        setup_pool = sem("setup_pool")
        x_loaded = sem("x_loaded")
        x_copied = sem("x_copied")
        out_ready = sem("out_ready")
        out_stored = sem("out_stored")

        xn_ready = sem("xn_ready")
        xt_psum = sem("xt_psum")
        xt_hi_ready = sem("xt_hi_ready")
        xt_lo_ready = sem("xt_lo_ready")
        qkv_psum = sem("qkv_psum")
        qkv_ready = sem("qkv_ready")
        sq_ready = sem("sq_ready")
        v_ready = sem("v_ready")
        qk_w_ready = sem("qk_w_ready")
        qk_hi_ready = sem("qk_hi_ready")
        qk_lo_ready = sem("qk_lo_ready")
        kt_psum = sem("kt_psum")
        qt_psum = sem("qt_psum")
        kt_ready = sem("kt_ready")
        qt_ready = sem("qt_ready")
        zeroed = sem("zeroed")
        qz_ready = [sem(f"qz_ready_{j}") for j in range(G0)]
        kz_ready = [sem(f"kz_ready_{j}") for j in range(2)]
        s_psum = sem("s_psum")
        max_done = sem("max_done")
        max_in_q = sem("max_in_q")
        qm_psum = sem("qm_psum")
        qm_ready = sem("qm_ready")
        st_psum = sem("st_psum")
        exp_done = sem("exp_done")
        pv_done = sem("pv_done")
        o_copied = sem("o_copied")
        on_psum = sem("on_psum")
        on_ready = sem("on_ready")
        ot_psum = sem("ot_psum")
        ot_hi_ready = sem("ot_hi_ready")
        ot_lo_ready = sem("ot_lo_ready")
        proj_psum = sem("proj_psum")

        xn2_ready = sem("xn2_ready")
        xt2_psum = sem("xt2_psum")
        x_tf_ready = sem("x_tf_ready")
        score_psum = sem("score_psum")
        scores_copied = sem("scores_copied")
        gate_exp_ready = sem("gate_exp_ready")
        gates_ready = sem("gates_ready")
        gt_psum = sem("gt_psum")
        gt_ready = sem("gt_ready")
        gate_psum = sem("gate_psum")
        gated = sem("gated")
        xg_hi_ready = sem("xg_hi_ready")
        xg_lo_ready = sem("xg_lo_ready")
        mid_psum = sem("mid_psum")
        sw_psum = sem("sw_psum")
        silu_done = sem("silu_done")
        h_done = sem("h_done")
        h_hi_ready = sem("h_hi_ready")
        h_lo_dve = sem("h_lo_dve")
        h_lo_pool = sem("h_lo_pool")
        expert_psum = sem("expert_psum")
        moe_copied = sem("moe_copied")
        moe_psum = sem("moe_psum")

        x_dup_ready = sem("x_dup_ready")
        xd_psum = sem("xd_psum")
        xd_hi_ready = sem("xd_hi_ready")
        xd_lo_ready = sem("xd_lo_ready")
        k_psum = sem("k_psum")
        k_hi_ready = sem("k_hi_ready")
        k_lo_ready = sem("k_lo_ready")
        v_psum = sem("v_psum")
        v1_ready = sem("v1_ready")
        q_psum = sem("q_psum")
        q_hi_ready = sem("q_hi_ready")
        q_lo_ready = sem("q_lo_ready")
        s1_psum = sem("s1_psum")
        att_ready = sem("att_ready")
        exp1_done = sem("exp1_done")
        rden_ready = sem("rden_ready")
        p_ready = sem("p_ready")
        pt_psum = sem("pt_psum")
        pt_a_ready = sem("pt_a_ready")
        pt_b_ready = sem("pt_b_ready")
        pv1_done = sem("pv1_done")
        o_hi_ready = sem("o_hi_ready")
        o_lo_ready = sem("o_lo_ready")
        wo_psum = sem("wo_psum")
        wo_copied = sem("wo_copied")
        x3_psum = sem("x3_psum")
        xn4_ready = sem("xn4_ready")
        xt4_psum = sem("xt4_psum")
        f_hi_ready = sem("f_hi_ready")
        f_lo_ready = sem("f_lo_ready")
        ffn_psum = sem("ffn_psum")
        trig_in = sem("trig_in")
        trig_out = sem("trig_out")
        alibi_masked = sem("alibi_masked")
        scores_seen = sem("scores_seen")
        rden_seen = sem("rden_seen")
        alibi_ready = sem("alibi_ready")
        rel_ready = sem("rel_ready")

        block = ctx.enter_context(nc.Block())

        @block.sync
        def _(sp):
            sp.dma_start(raw, w_all).then_inc(weights_in, 16)
            for dst, src in ((b_qkv_sb[:, :], b_qkv), (b_proj_sb[:, :], b_proj), (norm_w_raw[:, 0, :], qn_w),
                             (norm_w_raw[:, 1, :], kn_w)):
                sp.dma_start(dst, src.partition_broadcast(P)).then_inc(consts_in, 16)
            sp.dma_start(router_sb[:, :], router).then_inc(consts_in, 16)
            sp.dma_start(angle_sb[:, 0, :], angle.partition_broadcast(P)).then_inc(consts_in, 16)
            sp.dma_start(slope_sb[:, :], slopes.partition_broadcast(P)).then_inc(consts_in, 16)
            sp.sem_inc(out_stored, 16)
            sp.dma_start(x_in[:, :, :], x_dram[0]).then_inc(x_loaded, 16)

            def strips(b):
                def keys(g):
                    if g >= 2:
                        sp.wait_ge(st_psum, b * 32 + 8 * (g - 1))
                    for j in range(G0):
                        rows = slice(ROWS * j, ROWS * j + ROWS)
                        sp.dma_start(k_z[rows, g % 2, j, :].bitcast(F32), k_t[rows, g, :].bitcast(F32)).then_inc(kz_ready[g % 2], 16)

                def queries(h):
                    g, j = h // G0, h % G0
                    rows = slice(ROWS * j, ROWS * j + ROWS)
                    if g > 0:
                        sp.wait_ge(s_psum, b * H0 * NT + NT * (h - G0 + 1))
                    sp.dma_start(q_z[rows, j, :].bitcast(F32), q_t[rows, g, :].bitcast(F32)).then_inc(qz_ready[j], 16)

                sp.wait_ge(zeroed, b + 1)
                sp.wait_ge(qt_ready, b * NG + 1)
                for h in range(G0):
                    queries(h)
                sp.wait_ge(kt_ready, b * NG + 1)
                keys(0)
                sp.wait_ge(kt_ready, b * NG + NG)
                sp.wait_ge(qt_ready, b * NG + NG)
                queries(G0)
                keys(1)
                for h in range(G0 + 1, H0):
                    queries(h)
                    if h == 12:
                        keys(2)
                keys(3)

            if NB > 1:
                with sp.Fori(0, NB - 1) as b:
                    sp.wait_ge(xn_ready, b + 1)
                    sp.wait_ge(x_copied, b + 1)
                    sp.dma_start(x_in[:, :, :], x_dram[b + 1]).then_inc(x_loaded, 16)
                    strips(b)
                    sp.wait_ge(out_ready, b + 1)
                    sp.dma_start(out_dram[b], x_res[:, :, :]).then_inc(out_stored, 16)
            strips(NB - 1)
            sp.wait_ge(out_ready, NB)
            sp.dma_start(out_dram[NB - 1], x_res[:, :, :]).then_inc(out_stored, 16)
            sp.wait_ge(out_stored, 16 * NB + 16)

        @block.gpsimd
        def _(pool):
            pool.memset(ident[:, :], 0.0)
            pool.memset(v_nat[:, :, :], 0.0)
            pool.drain()
            pool.affine_select(out=ident[:, :], in_=ident[:, :], compare_op=ALU.not_equal, fill=1.0, base=0,
                               pattern=[[-1, P]], channel_multiplier=1)
            pool.iota(expert_ids[:, :], pattern=[[1, E]], base=0, channel_multiplier=0,
                      allow_small_or_imprecise_dtypes=True)
            v_heads = v_nat[:, :, 0:VW * H0].rearrange("p t (h d) -> p t h d", d=VW)
            pool.memset(v_heads[:, :, :, D0:VW], 1.0)
            pool.drain()
            pool.tensor_tensor(pick[:, :], ident[0:2 * E, 0:E], ident[0:2 * E, E:2 * E], ALU.add).then_inc(ident_ready, 1)
            pool.iota(x_res[:, :, :].rearrange("p t c -> p (t c)"), pattern=[[-1, T]], base=T - P,
                      channel_multiplier=1, allow_small_or_imprecise_dtypes=True).then_inc(rel_ready, 1)
            pool.wait_ge(alibi_ready, 1)
            pool.affine_select(out=alibi[:, :, T - P:T], in_=alibi[:, :, T - P:T], compare_op=ALU.is_ge, fill=-BIG,
                               base=0, pattern=[[0, H1], [-1, P]],
                               channel_multiplier=1).then_inc(alibi_masked, 1)
            with pool.Fori(0, NB) as b:
                pool.wait_ge(w_lo_ready, 1)
                pool.wait_ge(qkv_ready, b * NT + NT)
                pool.wait_ge(out_stored, b * 16 + 16)
                for t in range(NT):
                    pool.tensor_tensor(x_res[:, t, :], x_in[:, t, :], b_proj_sb[:, :], ALU.add)
                pool.memset(nat_q[:, :, :, AUG:ROWS], 0.0)
                pool.memset(nat_k[:, :, :, AUG + 2:ROWS], 0.0)
                pool.memset(nat_k[:, :, :, AUG:AUG + 2], 1.0).then_inc(x_copied, 1)
                pool.memset(q_z.bitcast(F32), 0.0)
                pool.memset(k_z.bitcast(F32), 0.0).then_inc(zeroed, 1)
                for t in range(NT):
                    m = pool.tensor_copy(v_heads[:, t, :, 0:D0],
                                         qkv[:, t, QK:3 * C].rearrange("p (h d) -> p h d", d=D0))
                m.then_inc(v_ready, 1)

                for k in range(NE):
                    pool.wait_ge(xg_hi_ready, b * NE + k + 1)
                    pool.tensor_tensor(xg_r[:, k % 2, 1, :], x_gated[:, k % 2, :] if k else x_tf,
                                       xg_r[:, k % 2, 0, :].bitcast(F32), ALU.subtract).then_inc(xg_lo_ready, 1)
                    if k > 0:
                        j = k - 1
                        pool.wait_ge(h_hi_ready, b * NE + j + 1)
                        pool.tensor_tensor(h_r[:, j % 2, 1, 1, :], hidden[:, j % 2, 1, :],
                                           h_r[:, j % 2, 0, 1, :].bitcast(F32), ALU.subtract).then_inc(h_lo_pool, 1)
                j = NE - 1
                pool.wait_ge(h_hi_ready, b * NE + j + 1)
                pool.tensor_tensor(h_r[:, j % 2, 1, 1, :], hidden[:, j % 2, 1, :],
                                   h_r[:, j % 2, 0, 1, :].bitcast(F32), ALU.subtract).then_inc(h_lo_pool, 1)

                for h in range(H1):
                    pool.wait_ge(rden_ready, b * H1 + h + 1)
                    pool.sem_inc(rden_seen, 1)
                    for i in range(NT):
                        p = att[:, h % 3, ROW_AT[i]:ROW_AT[i] + P * (i + 1)]
                        pool.tensor_scalar(p, p, rden[:, h, i:i + 1], 1.0, ALU.mult, ALU.mult).then_inc(p_ready, 1)

        @block.scalar
        def _(act):
            act.wait_ge(weights_in, 16)
            act.wait_ge(consts_in, 16 * 7)
            act.activation(slope_sb[:, :], slope_sb[:, :], ACT.Exp).then_inc(trig_out, 1)
            act.wait_ge(trig_in, 1)
            act.activation(angle_sb[:, 2, :], angle_sb[:, 1, :], ACT.Sin)
            act.activation(angle_sb[:, 3, :], angle_sb[:, 1, :], ACT.Sin, scale=0.5).then_inc(trig_out, 1)
            act.wait_ge(trig_in, 2)
            act.activation(raw[:, COL["sign"]:COL["sign"] + C], raw[:, COL["sign"]:COL["sign"] + C], ACT.Sign)
            act.drain()
            act.activation(w_hi[:, :], raw, ACT.Copy).then_inc(w_hi_ready, 1)
            with act.Fori(0, NB) as b:
                act.wait_ge(xt_psum, b + 1)
                act.activation(x_t[:, 0, :], bank(0), ACT.Copy).then_inc(xt_hi_ready, 1)
                for t in range(NT):
                    act.wait_ge(qkv_ready, b * NT + t + 1)
                    act.activation(qk_sq[:, t, :], qkv[:, t, 0:QK], ACT.Square).then_inc(sq_ready, 1)
                act.wait_ge(qk_w_ready, b + 1)
                qv = qk_w[:, :, 0:C].rearrange("p t (h d) -> p t h d", d=D0)
                kv = qk_w[:, :, C:QK].rearrange("p t (h d) -> p t h d", d=D0)
                for nat, src, at in ((nat_q, qv, 0), (nat_q, qv, 1), (nat_k, kv, 0), (nat_k, kv, 2)):
                    m = act.activation(nat[:, :, :, at * D0:at * D0 + D0].bitcast(F32R), src, ACT.Copy)
                m.then_inc(qk_hi_ready, 1)
                for g in range(NG):
                    act.wait_ge(kt_psum, b * NG + g + 1)
                    act.activation(k_t[:, g, :], bank(g), ACT.Copy).then_inc(kt_ready, 1)

                def copy_qm(g):
                    act.wait_ge(qm_psum, b * NG + g + 1)
                    act.activation(q_t[:, g, :], bank(7), ACT.Copy).then_inc(qm_ready, 1)

                def copy_o(g):
                    act.wait_ge(pv_done, b * 4 * NG + 4 * g + 4)
                    act.activation(o_t, bank(6), ACT.Copy).then_inc(o_copied, 1)

                act.wait_ge(v_ready, b + 1)
                copy_qm(0)
                for g in range(NG):
                    for kb in range(NT):
                        q = g * NT + kb
                        if q >= 2:
                            act.wait_ge(pv_done, b * 4 * NG + q - 1)
                        for half in range(2):
                            n = 2 * q + half
                            act.wait_ge(st_psum, b * 32 + n + 1)
                            act.activation(probs[:, q % 2, 2 * half:2 * half + 2, :],
                                           psum[:, 2 * half:2 * half + 2, :], ACT.Exp).then_inc(exp_done, 1)
                        if kb == 0 and g > 0:
                            copy_o(g - 1)
                    if g + 1 < NG:
                        copy_qm(g + 1)
                copy_o(NG - 1)
                act.wait_ge(ot_psum, b + 1)
                act.activation(a_t[:, 0, :], bank(0), ACT.Copy).then_inc(ot_hi_ready, 1)

                act.wait_ge(xt2_psum, b + 1)
                act.activation(x_tf, bank(0), ACT.Copy).then_inc(x_tf_ready, 1)
                act.activation(xg_r[:, 0, 0, :], bank(0), ACT.Copy).then_inc(xg_hi_ready, 1)
                act.wait_ge(scores_copied, b + 1)
                act.activation(gate_exp, scores_sb, ACT.Exp, scale=-1.0).then_inc(gate_exp_ready, 1)

                def silu_of(k):
                    act.wait_ge(mid_psum, b * NE + k + 1)
                    if k >= 2:
                        act.wait_ge(h_done, b * NE + k - 1)
                    act.activation(silu[:, k % 2, :, :], psum[:, 2:4, :], ACT.Silu).then_inc(silu_done, 1)

                for k in range(NE):
                    silu_of(k)
                    if k == 0:
                        act.wait_ge(gt_psum, b + 1)
                        act.activation(g_t[0:2 * E, :], bank(1)[0:2 * E, :], ACT.Copy).then_inc(gt_ready, 1)
                    if k + 1 < NE:
                        act.wait_ge(gated, b * E + k + 1)
                        if k >= 1:
                            act.wait_ge(sw_psum, b * NE + k)
                        act.activation(xg_r[:, (k + 1) % 2, 0, :], x_gated[:, (k + 1) % 2, :],
                                       ACT.Copy).then_inc(xg_hi_ready, 1)
                    act.wait_ge(h_done, b * NE + k + 1)
                    if k >= 2:
                        act.wait_ge(expert_psum, b * NE + k - 1)
                    act.activation(h_r[:, k % 2, 0, :, :], hidden[:, k % 2, :, :], ACT.Copy).then_inc(h_hi_ready, 1)
                act.wait_ge(expert_psum, b * NE + NE)
                act.activation(moe_t, bank(6), ACT.Copy).then_inc(moe_copied, 1)

                for j, dst in enumerate((tok_r, pos_r)):
                    act.wait_ge(xd_psum, b * 2 + j + 1)
                    act.activation(dst, bank(j), ACT.Copy).then_inc(xd_hi_ready, 1)
                for g in range(KVH):
                    act.wait_ge(k_psum, b * KVH + g + 1)
                    act.activation(k_r[:, g, 0, :], bank(2 + g), ACT.Copy).then_inc(k_hi_ready, 1)
                for j in range(2):
                    act.wait_ge(v_psum, b * 2 + j + 1)
                    act.activation(v1[:, 2 * j:2 * j + 2, :], bank(6 + j), ACT.Copy).then_inc(v1_ready, 1)

                def q_hi(h):
                    half = D1 * (h % 2)
                    act.wait_ge(q_psum, b * (H1 // 2) + h // 2 + 1)
                    act.activation(q_r[0:D1, h % 4, :], bank(0)[half:half + D1, :], ACT.Copy).then_inc(q_hi_ready, 1)

                q_hi(0)
                q_hi(1)
                for s in range(H1 + 4):
                    if s + 2 < H1:
                        q_hi(s + 2)
                    if s < H1:
                        for i in range(NT):
                            a = att[:, s % 3, ROW_AT[i]:ROW_AT[i] + P * (i + 1)]
                            act.wait_ge(att_ready, b * 4 * H1 + 4 * s + i + 1)
                            act.activation(a, a, ACT.Exp, bias=neg_m[:, s, i:i + 1], scale=-1.0,
                                           accum_out=sums[:, s, i:i + 1]).then_inc(exp1_done, 1)
                    h = s - 2
                    if 0 <= h < H1:
                        act.wait_ge(pt_psum, b * H1 + h + 1)
                        if h >= 4:
                            act.wait_ge(pv1_done, b * (H1 // 2) + (h - 4) // 2 + 1)
                        act.activation(probs_t[:, h % 4, 0:T], bank(3), ACT.Copy).then_inc(pt_a_ready, 1)
                    if s % 2 == 0 and s >= 4:
                        p = (s - 4) // 2
                        act.wait_ge(pv1_done, b * (H1 // 2) + p + 1)
                        if p >= 1:
                            act.wait_ge(wo_psum, b * (H1 // 2) + p)
                        act.activation(o_r[:, 0, 0, :], bank(6), ACT.Copy).then_inc(o_hi_ready, 1)
                act.wait_ge(wo_psum, b * (H1 // 2) + H1 // 2)
                act.activation(wo_t, bank(7), ACT.Copy).then_inc(wo_copied, 1)
                act.wait_ge(xt4_psum, b + 1)
                act.activation(f_r[:, 0, :], bank(1), ACT.Copy).then_inc(f_hi_ready, 1)

        @block.vector
        def _(dve):
            def rsqrt(y, var, tmp, eps):
                dve.tensor_scalar(var, var, eps, None, ALU.add)
                dve.drain()
                dve.tensor_scalar(tmp.bitcast(U32), var.bitcast(U32), 1, None, ALU.logical_shift_right)
                dve.drain()
                dve.tensor_scalar(y.bitcast(I32), tmp.bitcast(I32), -1.0, float(0x5F3759DF), ALU.mult, ALU.add)
                dve.drain()
                for _ in range(3):
                    dve.tensor_tensor(tmp, y, y, ALU.mult)
                    dve.drain()
                    dve.tensor_tensor(tmp, tmp, var, ALU.mult)
                    dve.drain()
                    dve.tensor_scalar(tmp, tmp, -0.5, 1.5, ALU.mult, ALU.add)
                    dve.drain()
                    dve.tensor_tensor(y, y, tmp, ALU.mult)
                    dve.drain()

            def layernorm_stats(src):
                for t in range(NT):
                    dve.bn_stats(stats[:, t, :], src[:, t, :])
                dve.drain()
                for t in range(NT):
                    dve.bn_aggr(mean_var[:, t, :], stats[:, t, :])
                dve.drain()
                dve.tensor_copy(newton[:, :], mean_var[:, :, 1])
                dve.drain()
                rsqrt(rstd[:, :], newton[:, :], rstd_tmp[:, :], LN_EPS)

            rstd_tmp = stats[:, :, 0]

            def normalise_x(src, dst):
                layernorm_stats(src)
                for t in range(NT):
                    m = dve.tensor_scalar(dst[:, t, :], src[:, t, :], mean_var[:, t, 0:1], rstd[:, t:t + 1],
                                          ALU.subtract, ALU.mult)
                return m

            def dve_l1(b):
                dve.drain()
                layernorm_stats(x_res)
                for t in range(NT):
                    m = dve.tensor_scalar(x_dup[:, t, :, :, :],
                                          x_res[:, t, :].rearrange("p (a c) -> p a c", a=2)[:, :, None, :].broadcast_to([P, 2, 2, D1]),
                                          mean_var[:, t, 0:1], rstd[:, t:t + 1], ALU.subtract, ALU.mult)
                m.then_inc(x_dup_ready, 1)
                low = slice(D1, P)
                for j, dst in enumerate((tok_r, pos_r)):
                    dve.wait_ge(xd_hi_ready, b * 2 + j + 1)
                    dve.tensor_tensor(dst[low, :], bank(j)[low, :], dst[low, :].bitcast(F32),
                                      ALU.subtract).then_inc(xd_lo_ready, 1)
                for g in range(KVH):
                    dve.wait_ge(k_hi_ready, b * KVH + g + 1)
                    dve.tensor_tensor(k_r[:, g, 1, :], bank(2 + g), k_r[:, g, 0, :].bitcast(F32),
                                      ALU.subtract).then_inc(k_lo_ready, 1)

                def q_lo(h):
                    half = D1 * (h % 2)
                    dve.wait_ge(q_hi_ready, b * H1 + h + 1)
                    dve.tensor_tensor(q_r[low, h % 4, :], bank(0)[half:half + D1, :],
                                      q_r[0:D1, h % 4, :].bitcast(F32), ALU.subtract).then_inc(q_lo_ready, 1)

                q_lo(0)
                q_lo(1)
                for s in range(H1 + 4):
                    if s + 2 < H1:
                        q_lo(s + 2)
                    if s < H1:
                        for i in range(NT):
                            n = 4 * s + i
                            w = P * (i + 1)
                            dve.wait_ge(s1_psum, b * 4 * H1 + n + 1)
                            dve.sem_inc(scores_seen, 1)
                            dve.tensor_tensor_reduce(att[:, s % 3, ROW_AT[i]:ROW_AT[i] + w], bank(1 + n % 2)[:, 0:w],
                                                     alibi[:, s, T - w:T], -1.0, BIG, ALU.add, ALU.min,
                                                     neg_m[:, s, i:i + 1]).then_inc(att_ready, 1)
                    h = s - 1
                    if 0 <= h < H1:
                        dve.wait_ge(exp1_done, b * 4 * H1 + 4 * h + 4)
                        dve.tensor_scalar(sums[:, h, :], sums[:, h, :], 1.0, None, ALU.add)
                        dve.drain()
                        dve.reciprocal(rden[:, h, :], sums[:, h, :]).then_inc(rden_ready, 1)
                    h = s - 2
                    if 0 <= h < H1:
                        dve.wait_ge(pt_psum, b * H1 + h + 1)
                        if h >= 4:
                            dve.wait_ge(pv1_done, b * (H1 // 2) + (h - 4) // 2 + 1)
                        dve.tensor_copy(probs_t[:, h % 4, T:CAUSAL],
                                        psum[:, 4:6, :].rearrange("p a c -> p (a c)")[:, 0:CAUSAL - T]).then_inc(pt_b_ready, 1)
                    if s % 2 == 0 and s >= 4:
                        p = (s - 4) // 2
                        dve.wait_ge(o_hi_ready, b * (H1 // 2) + p + 1)
                        dve.tensor_tensor(o_r[:, 0, 1, :], bank(6), o_r[:, 0, 0, :].bitcast(F32),
                                          ALU.subtract).then_inc(o_lo_ready, 1)
                dve.wait_ge(x3_psum, b + 1)
                flat = x_res[:, :, :].rearrange("p t c -> p (t c)")
                dve.tensor_tensor(flat, bank(0), flat, ALU.add)
                dve.drain()
                normalise_x(x_res, xn4).then_inc(xn4_ready, 1)
                dve.wait_ge(f_hi_ready, b + 1)
                dve.tensor_tensor(f_r[:, 1, :], bank(1), f_r[:, 0, :].bitcast(F32), ALU.subtract).then_inc(f_lo_ready, 1)
                dve.wait_ge(ffn_psum, b + 1)
                dve.tensor_tensor(flat, bank(2), flat, ALU.add).then_inc(out_ready, 1)

            def dve_moe(b):
                dve.drain()
                normalise_x(x_res, xn2).then_inc(xn2_ready, 1)
                dve.wait_ge(score_psum, b + 1)
                dve.tensor_copy(scores_sb, bank(1)[:, 0:NT * E].rearrange("p (t e) -> p t e", e=E)).then_inc(scores_copied, 1)
                dve.drain()
                for t in range(NT):
                    dve.max(top[:, t, :], scores_sb[:, t, :])
                dve.drain()
                for t in range(NT):
                    dve.max_index(top_at[:, t, :].bitcast(U32), top[:, t, :], scores_sb[:, t, :])
                dve.drain()
                dve.tensor_copy(top_atf, top_at[:, :, 0:2].bitcast(U32))
                dve.drain()
                for j in range(2):
                    dve.tensor_tensor(chosen[:, j, :, :], expert_ids[:, None, :].broadcast_to([P, NT, E]),
                                      top_atf[:, :, j:j + 1].broadcast_to([P, NT, E]), ALU.is_equal)
                dve.wait_ge(gate_exp_ready, b + 1)
                dve.tensor_scalar(gate_exp, gate_exp, 1.0, None, ALU.add)
                dve.drain()
                dve.reciprocal(gate, gate_exp)
                dve.tensor_tensor(chosen[:, 0, :, :], chosen[:, 0, :, :], chosen[:, 1, :, :], ALU.add)
                dve.drain()
                dve.tensor_tensor(gate, gate, chosen[:, 0, :, :], ALU.mult)
                dve.drain()
                dve.tensor_copy(gates_nat[:, :, 0:E].bitcast(F32R), gate)
                dve.drain()
                dve.tensor_tensor(gates_nat[:, :, E:2 * E], gate, gates_nat[:, :, 0:E], ALU.subtract).then_inc(gates_ready, 1)

                def gate_x(k):
                    dve.wait_ge(gate_psum, b * E + k)
                    if k >= 3:
                        dve.wait_ge(xg_lo_ready, b * NE + k - 1)
                    dve.tensor_tensor(x_gated[:, k % 2, :], bank(7), x_tf, ALU.mult).then_inc(gated, 1)

                gate_x(1)
                for k in range(NE):
                    dve.wait_ge(sw_psum, b * NE + k + 1)
                    dve.wait_ge(silu_done, b * NE + k + 1)
                    if k >= 2:
                        dve.wait_ge(h_lo_pool, b * NE + k - 1)
                    dve.tensor_tensor(hidden[:, k % 2, :, :], psum[:, 4:6, :], silu[:, k % 2, :, :],
                                      ALU.mult).then_inc(h_done, 1)
                    if 1 <= k + 2 < NE:
                        gate_x(k + 2)
                    dve.wait_ge(h_hi_ready, b * NE + k + 1)
                    dve.tensor_tensor(h_r[:, k % 2, 1, 0, :], hidden[:, k % 2, 0, :],
                                      h_r[:, k % 2, 0, 0, :].bitcast(F32), ALU.subtract).then_inc(h_lo_dve, 1)
                dve.wait_ge(moe_psum, b + 1)
                dve.tensor_tensor(x_res[:, :, :].rearrange("p t c -> p (t c)"), bank(0),
                                  x_res[:, :, :].rearrange("p t c -> p (t c)"), ALU.add)
                dve_l1(b)
            dve.wait_ge(consts_in, 16 * 7)
            dve.tensor_copy(norm_w[:, :, :, :], norm_w_raw[:, :, None, :].broadcast_to([P, 2, H0, D0]))
            dve.drain()
            dve.tensor_scalar(norm_w[:, 0, :, :], norm_w[:, 0, :, :], D0 ** -0.5, None, ALU.mult)
            scratch = alibi[:, 0:2, :].rearrange("p a c -> p (a c)")
            turns = scratch[:, 0:H1]
            dve.tensor_scalar(turns, angle_sb[:, 0, :], 1.0 / (2 * math.pi), None, ALU.mult)
            dve.drain()
            dve.tensor_copy(scratch[:, 64:64 + H1].bitcast(I32), turns)
            dve.drain()
            dve.tensor_copy(turns, scratch[:, 64:64 + H1].bitcast(I32))
            dve.drain()
            for part in TURN:
                dve.tensor_scalar(scratch[:, 128:128 + H1], turns, -part, None, ALU.mult)
                dve.drain()
                dve.tensor_tensor(angle_sb[:, 0, :], angle_sb[:, 0, :], scratch[:, 128:128 + H1], ALU.add)
                dve.drain()
            dve.tensor_scalar(angle_sb[:, 1, :], angle_sb[:, 0, :], PI_DOWN, -PI_DOWN, ALU.min, ALU.max).then_inc(trig_in, 1)
            dve.wait_ge(trig_out, 2)
            dve.tensor_tensor(angle_sb[:, 3, :], angle_sb[:, 3, :], angle_sb[:, 3, :], ALU.mult)
            dve.drain()
            dve.tensor_scalar(angle_sb[:, 3, :], angle_sb[:, 3, :], -2 * D1 ** -0.5, D1 ** -0.5, ALU.mult, ALU.add)
            dve.tensor_scalar(angle_sb[:, 2, :], angle_sb[:, 2, :], D1 ** -0.5, None, ALU.mult)
            dve.drain()
            dve.wait_ge(weights_in, 16)
            pairs = raw[:, COL["wq"]:COL["wq"] + H1 * D1].rearrange("p (h d two) -> p two h d", h=H1, two=2)
            sin_a = angle_sb[:, 2, :][:, :, None].broadcast_to([P, H1, D1 // 2])
            cos_a = angle_sb[:, 3, :][:, :, None].broadcast_to([P, H1, D1 // 2])
            terms = [alibi[:, 4 + j, :].rearrange("p (h d) -> p h d", h=H1) for j in range(4)]
            for term, side, turn in zip(terms, (0, 1, 0, 1), (cos_a, sin_a, sin_a, cos_a)):
                dve.tensor_tensor(term, pairs[:, side], turn, ALU.mult)
            dve.drain()
            dve.tensor_tensor(pairs[:, 0], terms[0], terms[1], ALU.subtract)
            dve.tensor_tensor(pairs[:, 1], terms[2], terms[3], ALU.add).then_inc(trig_in, 1)
            dve.drain()
            dve.wait_ge(rel_ready, 1)
            dve.wait_ge(trig_out, 2)
            for h in range(H1):
                m = dve.tensor_scalar(alibi[:, h, :], x_res[:, :, :].rearrange("p t c -> p (t c)"),
                                      slope_sb[:, h:h + 1], None, ALU.mult)
            m.then_inc(alibi_ready, 1)
            dve.wait_ge(w_hi_ready, 1)
            dve.tensor_tensor(w_lo[:, :], raw, w_hi[:, :].bitcast(F32), ALU.subtract).then_inc(w_lo_ready, 1)
            dve.drain()
            dve.wait_ge(alibi_masked, 1)
            with dve.Fori(0, NB) as b:
                dve.wait_ge(x_loaded, b * 16 + 16)
                layernorm_stats(x_in)
                for t in range(NT):
                    m = dve.tensor_scalar(xn[:, t, :], x_in[:, t, :], mean_var[:, t, 0:1], rstd[:, t:t + 1],
                                          ALU.subtract, ALU.mult)
                m.then_inc(xn_ready, 1)
                dve.wait_ge(xt_hi_ready, b + 1)
                dve.tensor_tensor(x_t[:, 1, :], bank(0), x_t[:, 0, :].bitcast(F32),
                                  ALU.subtract).then_inc(xt_lo_ready, 1)
                for t in range(NT):
                    dve.wait_ge(qkv_psum, b * NT + t + 1)
                    dve.tensor_tensor(qkv[:, t, :], bank(1 + t)[:, 0:3 * C], b_qkv_sb[:, :],
                                      ALU.add).then_inc(qkv_ready, 1)
                dve.wait_ge(sq_ready, b * NT + NT)
                dve.tensor_reduce(ms, qk_sq.rearrange("p t (h d) -> p (t h) d", d=D0), AX.X, ALU.add)
                dve.drain()
                dve.tensor_scalar(ms, ms, 1.0 / D0, None, ALU.mult)
                dve.drain()
                rsqrt(ms_y, ms, ms_t, RMS_EPS)
                for t in range(NT):
                    dve.tensor_tensor(qk_w[:, t, :].rearrange("p (h d) -> p h d", d=D0),
                                      qkv[:, t, 0:QK].rearrange("p (h d) -> p h d", d=D0),
                                      ms_y[:, t, :][:, :, None].broadcast_to([P, 2 * H0, D0]), ALU.mult)
                dve.drain()
                m = dve.tensor_tensor(qk_w, qk_w,
                                      norm_w[:, :, :, :].rearrange("p a h d -> p (a h d)")[:, None, :].broadcast_to([P, NT, QK]),
                                      ALU.mult)
                m.then_inc(qk_w_ready, 1)
                qv = qk_w[:, :, 0:C].rearrange("p t (h d) -> p t h d", d=D0)
                kv = qk_w[:, :, C:QK].rearrange("p t (h d) -> p t h d", d=D0)
                dve.wait_ge(qk_hi_ready, b + 1)
                dve.tensor_tensor(nat_q[:, :, :, 2 * D0:3 * D0], qv, nat_q[:, :, :, 0:D0], ALU.subtract)
                dve.tensor_tensor(nat_k[:, :, :, D0:2 * D0], kv, nat_k[:, :, :, 0:D0],
                                  ALU.subtract).then_inc(qk_lo_ready, 1)
                for g in range(NG):
                    dve.wait_ge(qt_psum, b * NG + g + 1)
                    dve.tensor_copy(q_t[:, g, :], bank(4 + g)).then_inc(qt_ready, 1)

                def head_max(h):
                    for i in range(NT):
                        n = h * NT + i
                        dve.wait_ge(s_psum, b * 64 + n + 1)
                        dve.tensor_reduce(neg_max[:, i, h:h + 1], bank(4 + n % 2), AX.X, ALU.max,
                                          negate=True).then_inc(max_done, 1)

                def split_max(g):
                    hs = slice(G0 * g, G0 * g + G0)
                    dve.drain()
                    dve.tensor_copy(nat_q[:, :, hs, AUG].bitcast(F32R), neg_max[:, :, hs])
                    dve.drain()
                    dve.tensor_tensor(nat_q[:, :, hs, AUG + 1], neg_max[:, :, hs], nat_q[:, :, hs, AUG],
                                      ALU.subtract).then_inc(max_in_q, 1)

                def normalise(g):
                    ob = bank(7).rearrange("p (t r d) -> p t r d", t=NT, r=G0)
                    dve.wait_ge(on_psum, b * NG + g + 1)
                    dve.reciprocal(rec, ob[:, :, :, D0])
                    dve.drain()
                    dve.tensor_tensor(o_nat[:, :, G0 * D0 * g:G0 * D0 * (g + 1)].rearrange("p t (r d) -> p t r d", r=G0),
                                      ob[:, :, :, 0:D0], rec[:, :, :, None].broadcast_to([P, NT, G0, D0]),
                                      ALU.mult).then_inc(on_ready, 1)

                for h in range(LEAD):
                    head_max(h)
                    if h % G0 == G0 - 1:
                        split_max(h // G0)
                for q in range(H0):
                    if q + LEAD < H0:
                        head_max(q + LEAD)
                        if (q + LEAD) % G0 == G0 - 1:
                            split_max((q + LEAD) // G0)
                    if q % NT == 1 and q > NT:
                        normalise(q // NT - 1)
                normalise(NG - 1)
                dve.wait_ge(ot_hi_ready, b + 1)
                dve.tensor_tensor(a_t[:, 1, :], bank(0), a_t[:, 0, :].bitcast(F32),
                                  ALU.subtract).then_inc(ot_lo_ready, 1)
                dve.wait_ge(proj_psum, b + 1)
                dve.wait_ge(x_copied, b + 1)
                dve.tensor_tensor(x_res[:, :, :].rearrange("p t c -> p (t c)"), bank(1),
                                  x_res[:, :, :].rearrange("p t c -> p (t c)"), ALU.add)
                dve_moe(b)

        @block.tensor
        def _(pe):
            def transposes(to, tiles):
                for t, tile in enumerate(tiles):
                    m = pe.transpose(to[:, P * t:P * t + P], tile, ident[:, :])
                return m

            def product(to, left, right, start=True, stop=True):
                (lh, ll), (rh, rl) = left, right
                pe.matmul(to, lh, rh, start=start, stop=False)
                pe.matmul(to, lh, rl, start=False, stop=False)
                return pe.matmul(to, ll, rh, start=False, stop=stop)

            def pe_l1(b):
                pe.wait_ge(x_dup_ready, b + 1)
                for j in range(2):
                    transposes(bank(j), [x_dup[:, t, j, :, :] for t in range(NT)]).then_inc(xd_psum, 1)

                def head(part, n, to):
                    pe.matmul(to, whi(part, P * n, P), pos_r, start=True, stop=False)
                    return pe.matmul(to, wlo(part, P * n, P), pos_r, start=False, stop=True)

                pe.wait_ge(xd_lo_ready, b * 2 + 2)
                for g in range(KVH):
                    head("wk", g, bank(2 + g)).then_inc(k_psum, 1)
                for t in range(NT):
                    to = bank(6 + t // 2)[:, KVH * D1 * (t % 2):KVH * D1 * (t % 2 + 1)]
                    pe.matmul(to, tok_r[:, P * t:P * t + P], whi("wv", 0, KVH * D1), start=True, stop=False)
                    m = pe.matmul(to, tok_r[:, P * t:P * t + P], wlo("wv", 0, KVH * D1), start=False, stop=True)
                    if t % 2:
                        m.then_inc(v_psum, 1)

                def queries(p):
                    if p > 0:
                        pe.wait_ge(q_lo_ready, b * H1 + 2 * p)
                    head("wq", p, bank(0)).then_inc(q_psum, 1)

                def scores1(h, i):
                    n, w = 4 * h + i, P * (i + 1)
                    if i == 0:
                        pe.wait_ge(q_lo_ready, b * H1 + h + 1)
                    if n >= 2:
                        pe.wait_ge(att_ready, b * 4 * H1 + n - 1)
                    q = q_r[:, h % 4, P * i:P * i + P]
                    pe.matmul(bank(1 + n % 2)[:, 0:w], q, k_r[:, h // REP, 0, 0:w], start=True, stop=False)
                    pe.matmul(bank(1 + n % 2)[:, 0:w], q, k_r[:, h // REP, 1, 0:w],
                              start=False, stop=True).then_inc(s1_psum, 1)

                def turn_p(h, i):
                    if i == 0 and h > 0:
                        pe.wait_ge(pt_a_ready, b * H1 + h)
                        pe.wait_ge(pt_b_ready, b * H1 + h)
                    pe.wait_ge(p_ready, b * 4 * H1 + 4 * h + i + 1)
                    to = psum[:, 3:6, :].rearrange("p a c -> p (a c)")
                    for j in range(i + 1):
                        at = KEY_AT[j] + P * (i - j)
                        m = pe.transpose(to[:, at:at + P], att[:, h % 3, ROW_AT[i] + P * j:ROW_AT[i] + P * j + P],
                                         ident[:, :])
                    if i == NT - 1:
                        m.then_inc(pt_psum, 1)

                def weigh1(p):
                    pe.wait_ge(pt_a_ready, b * H1 + 2 * p + 2)
                    pe.wait_ge(pt_b_ready, b * H1 + 2 * p + 2)
                    if p > 0:
                        pe.wait_ge(o_lo_ready, b * (H1 // 2) + p)
                    g = 2 * p // REP
                    for j in range(NT):
                        for e in range(2):
                            m = pe.matmul(bank(6)[D1 * e:D1 * e + D1, P * j:T], v1[:, j, D1 * g:D1 * g + D1],
                                          probs_t[:, (2 * p + e) % 4, KEY_AT[j]:KEY_AT[j] + T - P * j],
                                          start=(j == 0), stop=(j == NT - 1))
                    m.then_inc(pv1_done, 1)

                def project(p):
                    pe.wait_ge(o_lo_ready, b * (H1 // 2) + p + 1)
                    product(bank(7), (whi("wo", C * p, C), wlo("wo", C * p, C)), (o_r[:, 0, 0, :], o_r[:, 0, 1, :]),
                            start=(p == 0), stop=(p == H1 // 2 - 1)).then_inc(wo_psum, 1)

                queries(0)
                pe.wait_ge(k_lo_ready, b * KVH + KVH)
                pe.wait_ge(v1_ready, b * 2 + 2)
                for s in range(H1 + 4):
                    if s % 2 == 0 and s + 2 < H1:
                        queries(s // 2 + 1)
                    for i in range(NT):
                        if s < H1:
                            scores1(s, i)
                        if 0 <= s - 2 < H1:
                            turn_p(s - 2, i)
                    if s % 2 == 0 and s >= 4:
                        weigh1((s - 4) // 2)
                    if s % 2 == 1 and s >= 5:
                        project((s - 5) // 2)
                pe.wait_ge(wo_copied, b + 1)
                transposes(bank(0), [wo_t[:, P * t:P * t + P] for t in range(NT)]).then_inc(x3_psum, 1)
                pe.wait_ge(xn4_ready, b + 1)
                transposes(bank(1), [xn4[:, t, :] for t in range(NT)]).then_inc(xt4_psum, 1)
                pe.wait_ge(f_lo_ready, b + 1)
                for t in range(NT):
                    ts = slice(P * t, P * t + P)
                    pe.matmul(bank(2)[:, ts], f_r[:, 0, ts], whi("sign", 0, C), start=True, stop=False)
                    m = pe.matmul(bank(2)[:, ts], f_r[:, 1, ts], whi("sign", 0, C), start=False, stop=True)
                m.then_inc(ffn_psum, 1)

            def pe_moe(b):
                pe.wait_ge(xn2_ready, b + 1)
                transposes(bank(0), [xn2[:, t, :] for t in range(NT)]).then_inc(xt2_psum, 1)
                pe.wait_ge(x_tf_ready, b + 1)
                for t in range(NT):
                    m = pe.matmul(bank(1)[:, E * t:E * t + E], x_tf[:, P * t:P * t + P], router_sb[:, :],
                                  start=True, stop=True)
                m.then_inc(score_psum, 1)

                def up(part, e, ft, k, to):
                    at = e * F + P * ft
                    return product(to, (whi(part, at, P), wlo(part, at, P)),
                                   (xg_r[:, k % 2, 0, :], xg_r[:, k % 2, 1, :]))

                def gate_of(k):
                    if k >= 2:
                        pe.wait_ge(gated, b * E + k - 1)
                    pe.matmul(bank(7), pick[:, k - 1:k].broadcast_to([2 * E, P]), g_t[0:2 * E, :],
                              start=True, stop=True).then_inc(gate_psum, 1)

                def down(k):
                    e = order[k]
                    pe.wait_ge(h_lo_dve, b * NE + k + 1)
                    pe.wait_ge(h_lo_pool, b * NE + k + 1)
                    for ft in range(FT):
                        at = (e * FT + ft) * C
                        m = product(bank(6), (whi("wout", at, C), wlo("wout", at, C)),
                                    (h_r[:, k % 2, 0, ft, :], h_r[:, k % 2, 1, ft, :]),
                                    start=(k == 0 and ft == 0), stop=(k == NE - 1 and ft == FT - 1))
                    m.then_inc(expert_psum, 1)

                order = [E] + list(range(E))
                for k, e in enumerate(order):
                    pe.wait_ge(xg_lo_ready, b * NE + k + 1)
                    if k > 0:
                        pe.wait_ge(silu_done, b * NE + k)
                    for ft in range(FT):
                        m = up("win", e, ft, k, bank(2 + ft))
                    m.then_inc(mid_psum, 1)
                    if k == 0:
                        pe.wait_ge(gates_ready, b + 1)
                        transposes(bank(1)[0:2 * E, :], [gates_nat[:, t, :] for t in range(NT)]).then_inc(gt_psum, 1)
                    if k > 0:
                        pe.wait_ge(h_done, b * NE + k)
                    for ft in range(FT):
                        m = up("wsw", e, ft, k, bank(4 + ft))
                    m.then_inc(sw_psum, 1)
                    if k == 0:
                        pe.wait_ge(gt_ready, b + 1)
                        gate_of(1)
                    if k + 2 < NE:
                        gate_of(k + 2)
                    if k > 0:
                        down(k - 1)
                down(NE - 1)
                pe.wait_ge(moe_copied, b + 1)
                transposes(bank(0), [moe_t[:, P * t:P * t + P] for t in range(NT)]).then_inc(moe_psum, 1)
                pe_l1(b)

            pe.wait_ge(ident_ready, 1)
            pe.wait_ge(w_lo_ready, 1)
            with pe.Fori(0, NB) as b:
                pe.wait_ge(xn_ready, b + 1)
                transposes(bank(0), [xn[:, t, :] for t in range(NT)]).then_inc(xt_psum, 1)
                pe.wait_ge(xt_lo_ready, b + 1)
                for t in range(NT):
                    ts = slice(P * t, P * t + P)
                    product(bank(1 + t)[:, 0:3 * C], (x_t[:, 0, ts], x_t[:, 1, ts]),
                            (whi("qkv", 0, 3 * C), wlo("qkv", 0, 3 * C))).then_inc(qkv_psum, 1)
                pe.wait_ge(qk_lo_ready, b + 1)
                pe.wait_ge(x_copied, b + 1)
                for g in range(NG):
                    transposes(bank(g), [nat_k[:, t, G0 * g:G0 * g + G0, :] for t in range(NT)]).then_inc(kt_psum, 1)
                for g in range(NG):
                    transposes(bank(4 + g), [nat_q[:, t, G0 * g:G0 * g + G0, :] for t in range(NT)]).then_inc(qt_psum, 1)

                def scores(h, tiles):
                    g = h // G0
                    for i in tiles:
                        n = h * NT + i
                        if n >= 2:
                            pe.wait_ge(max_done, b * 64 + n - 1)
                        if i == 0:
                            pe.wait_ge(qz_ready[h % G0], b * 16 * NG + 16 * (g + 1))
                        pe.matmul(bank(4 + n % 2), q_z[:, h % G0, P * i:P * i + P], k_t[:, g, :],
                                  start=True, stop=True).then_inc(s_psum, 1)

                def scores_t(q, half):
                    g, kb = q // NT, q % NT
                    n = 2 * q + half
                    if n >= 2:
                        pe.wait_ge(exp_done, b * 32 + n - 1)
                    if n % (2 * NT) == 0:
                        pe.wait_ge(kz_ready[g % 2], (b * (NG // 2) + g // 2 + 1) * 16 * G0)
                    for j in range(2 * half, 2 * half + 2):
                        m = pe.matmul(bank(j), k_z[:, g % 2, j, P * kb:P * kb + P], q_t[:, g, :],
                                      start=True, stop=True)
                    m.then_inc(st_psum, 1)

                def weigh(q):
                    g, kb = q // NT, q % NT
                    pe.wait_ge(exp_done, b * 32 + 2 * q + 2)
                    if kb == 0 and g > 0:
                        pe.wait_ge(o_copied, b * NG + g)
                    if q == 0:
                        pe.wait_ge(v_ready, b + 1)
                    for j in range(G0):
                        r = ROWS * j
                        m = pe.matmul(bank(6)[r:r + ROWS, :], v_nat[:, kb, VW * (G0 * g + j):VW * (G0 * g + j) + ROWS], probs[:, q % 2, j, :],
                                      start=(kb == 0), stop=(kb == NT - 1))
                    m.then_inc(pv_done, 1)

                def turn_q(g):
                    pe.wait_ge(max_in_q, b * NG + g + 1)
                    if g >= 2:
                        pe.wait_ge(on_ready, b * NG + g - 1)
                    elif g == 1:
                        pe.wait_ge(qm_ready, b * NG + 1)
                    transposes(bank(7), [nat_q[:, t, G0 * g:G0 * g + G0, :] for t in range(NT)]).then_inc(qm_psum, 1)

                def turn_o(g):
                    pe.wait_ge(o_copied, b * NG + g + 1)
                    if g > 0:
                        pe.wait_ge(on_ready, b * NG + g)
                    pe.wait_ge(qm_ready, b * NG + min(g + 2, NG))
                    transposes(bank(7), [o_t[:, P * t:P * t + P] for t in range(NT)]).then_inc(on_psum, 1)

                pe.wait_ge(kt_ready, b * NG + NG)
                pe.wait_ge(qt_ready, b * NG + NG)
                for h in range(G0):
                    scores(h, range(NT))
                scores(G0, range(NT))
                turn_q(0)
                pe.wait_ge(qm_ready, b * NG + 1)
                for q in range(H0):
                    g, kb = q // NT, q % NT
                    h = q + LEAD
                    if kb == 0 and g > 0:
                        pe.wait_ge(qm_ready, b * NG + g + 1)
                    if h < H0:
                        scores(h, (0, 1))
                    scores_t(q, 0)
                    if h < H0:
                        scores(h, (2,))
                    scores_t(q, 1)
                    if h < H0:
                        scores(h, (3,))
                    if kb == NT - 1 and g + 1 < NG:
                        turn_q(g + 1)
                    if q > 0:
                        weigh(q - 1)
                    if kb == 1 and g > 0:
                        turn_o(g - 1)
                weigh(H0 - 1)
                turn_o(NG - 1)
                pe.wait_ge(on_ready, b * NG + NG)
                transposes(bank(0), [o_nat[:, t, :] for t in range(NT)]).then_inc(ot_psum, 1)
                pe.wait_ge(ot_lo_ready, b + 1)
                for t in range(NT):
                    ts = slice(P * t, P * t + P)
                    m = product(bank(1)[:, ts], (a_t[:, 0, ts], a_t[:, 1, ts]), (whi("proj", 0, C), wlo("proj", 0, C)))
                m.then_inc(proj_psum, 1)
                pe_moe(b)


def layout(g):
    import numpy as np
    w = np.zeros((P, NW), np.float32)

    def put(part, a):
        w[:, COL[part]:COL[part] + a.shape[1]] = a

    put("qkv", g["L0_attn_w_qkv"].T)
    put("proj", g["L0_attn_w_proj"].T)
    for e in range(E):
        w[:, COL["win"] + F * e:COL["win"] + F * (e + 1)] = g["L0_ffn_w_in_eDF"][e]
        w[:, COL["wsw"] + F * e:COL["wsw"] + F * (e + 1)] = g["L0_ffn_w_swiglu_eDF"][e]
    w[:, COL["win"] + F * E:COL["win"] + F * NE] = g["L0_ffn_w_in_shared_FD"].T
    w[:, COL["wsw"] + F * E:COL["wsw"] + F * NE] = g["L0_ffn_w_swiglu_FD"].T
    wout = np.concatenate([g["L0_ffn_w_out_eFD"], g["L0_ffn_w_out_shared_DF"].T[None]], 0)
    put("wout", wout.reshape(NE, FT, P, C).transpose(2, 0, 1, 3).reshape(P, NE * FT * C))
    ins = {"x": g["L0_attn_x"], "w_all": w, "b_qkv": g["L0_attn_b_qkv"], "b_proj": g["L0_attn_b_proj"],
           "qn_w": g["L0_attn_qn_w"], "kn_w": g["L0_attn_kn_w"], "router": g["L0_ffn_router_DE"],
           "angle": g["L1_attn_q_phase_angle"], "slopes": g["L1_attn_alibi_log_slopes"]}
    twice = lambda a: np.concatenate([a, a], 0)
    put("wq", twice(g["L1_attn_Wq"]))
    put("wk", twice(np.repeat(g["L1_attn_Wk"].reshape(-1, KVH, 1, D1), 2, 2).reshape(-1, 2 * KVH * D1)))
    put("wv", twice(g["L1_attn_Wv"]))
    put("wo", g["L1_attn_Wo"].reshape(H1 * D1 // P, P, C).transpose(1, 0, 2).reshape(P, -1))
    put("sign", g["L1_ffn_weight"].T)
    return ins


def kernel(**inputs):
    import numpy as np
    import concourse.bacc as bacc
    from concourse.bass_utils import run_bass_kernel_spmd

    arrays = layout({name: np.asarray(a) for name, a in inputs.items()})
    nc = bacc.Bacc("TRN2", target_bir_lowering=False, num_devices=1)
    aps = {name: nc.dram_tensor(f"in_{name}", a.shape, mybir.dt.from_np(a.dtype), kind="ExternalInput").ap()
           for name, a in arrays.items()}
    out = nc.dram_tensor("out", arrays["x"].shape, F32, kind="ExternalOutput").ap()
    kernel_program(nc, out=out, **aps)
    result = run_bass_kernel_spmd(nc, [{f"in_{name}": a for name, a in arrays.items()}], core_ids=[0])
    return result.results[0]["out"]
```

```python
from contextlib import ExitStack
import math

import concourse.bass as bass
from concourse import mybir

F32 = mybir.dt.float32
F32R = mybir.dt.float32r
I32 = mybir.dt.int32
U32 = mybir.dt.uint32
ALU = mybir.AluOpType
ACT = mybir.ActivationFunctionType
AX = mybir.AxisListType

P = 128
C = 128
T = 512
NT = T // P

H0, D0 = 16, 8
G0 = 4
NG = H0 // G0
ROWS = P // G0
AUG = 3 * D0
QK = 2 * C
VW = D0 + 1
LEAD = 5

E, F = 8, 256
NE = E + 1
FT = F // P

H1, D1, KVH = 16, 64, 4
REP = H1 // KVH
CAUSAL = P * NT * (NT + 1) // 2
ROW_AT = [P * i * (i + 1) // 2 for i in range(NT)]
KEY_AT = [0, 512, 1024, 896]
TILES = (3, 2, 0, 1)
SCORE_AT = {3: (1, 0, 4), 2: (2, 0, 3), 0: (2, 384, 3), 1: (1, 0, 4)}
LN_AT = 2
TURN = (6.28125, 2 * math.pi - 6.28125)
PI_DOWN = 3.1415925
LN_EPS, RMS_EPS = 1e-5, 1e-6
BIG = 3.0e38

PARTS = [("qkv", 3 * C), ("proj", C), ("win", NE * F), ("wsw", NE * F), ("wout", NE * F), ("wq", H1 * D1),
         ("wk", 2 * KVH * D1), ("wv", KVH * D1), ("wo", H1 * D1 // P * C), ("sign", C)]
COL = {}
NW = 0
for _name, _n in PARTS:
    COL[_name] = NW
    NW += _n


def kernel_program(nc, x, w_all, b_qkv, b_proj, qn_w, kn_w, router, angle, slopes, out):
    NB = x.shape[0]
    x_dram = x.rearrange("b (t p) c -> b p t c", p=P)
    out_dram = out.rearrange("b (t p) c -> b p t c", p=P)

    with ExitStack() as ctx:
        def sb(name, shape, dt=F32):
            return ctx.enter_context(nc.sbuf_tensor(name, shape, dt))

        def sem(name):
            return ctx.enter_context(nc.semaphore(name))

        w_hi = sb("w_hi", [P, NW], F32R)
        w_lo = sb("w_lo", [P, NW], F32R)
        ident = sb("ident", [P, P])
        b_qkv_sb = sb("b_qkv_sb", [P, 3 * C])
        b_proj_sb = sb("b_proj_sb", [P, C])
        norm_w_raw = sb("norm_w_raw", [P, 2, D0])
        q_weight = sb("q_weight", [P, H0, D0])
        router_sb = sb("router_sb", [P, E])
        x_in = sb("x_in", [P, NT, C])
        x_res = sb("x_res", [P, NT, C])
        v_mem = sb("v_mem", [P, NT * (VW * H0 + ROWS - VW)])
        expert_ids = sb("expert_ids", [P, E])
        pick = sb("pick", [2 * E, E], F32R)
        alibi = sb("alibi", [P, H1, T])
        angle_sb = sb("angle_sb", [P, 4, H1])
        slope_sb = sb("slope_sb", [P, H1])
        neg_m = sb("neg_m", [P, H1, NT])
        sums = sb("sums", [P, H1, NT])
        rden = sb("rden", [P, H1, NT])
        stats = sb("stats", [P, NT, 6])
        mean_var = sb("mean_var", [P, NT, 2])
        rstd = sb("rstd", [P, NT])
        half_var = sb("half_var", [P, NT])
        shared = sb("shared", [P, 11008])
        shared_r = sb("shared_r", [P, 10240], F32R)

        def carve(arena, at, *shape):
            n = math.prod(shape)
            ap = arena[:, at:at + n]
            names = "abcd"[:len(shape)]
            if len(shape) == 1:
                return ap
            return ap.rearrange(f"p ({' '.join(names)}) -> p {' '.join(names)}", **dict(zip(names, shape)))

        raw = shared[:, 0:NW]
        nat_q = carve(shared, 0, NT, H0, ROWS)
        nat_k = carve(shared, 2048, NT, H0, ROWS)
        probs = carve(shared, 4096, 2, G0, T)
        qkv = carve(shared, 4608, NT, 3 * C)
        qk_sq = carve(shared, 6144, NT, QK)
        qk_w = carve(shared, 8192, NT, QK)
        o_t = carve(shared, 9216, T)
        o_nat = carve(shared, 9728, NT, C)
        root_y = carve(shared, 10372, NT + NT * 2 * H0)
        root_tmp = carve(shared, 10504, NT + NT * 2 * H0)
        root_half = carve(shared, 10240, NT + NT * 2 * H0)
        ms = root_half[:, NT:]
        ms_y = root_y[:, NT:].rearrange("p (t h) -> p t h", t=NT)
        neg_max = carve(shared, 10768, NT, H0)
        rec = carve(shared, 10832, NT, G0)
        x_t = carve(shared_r, 0, 2, T)
        q_z = carve(shared_r, 0, G0, T)
        k_t = carve(shared_r, 2048, NG, T)
        q_t = carve(shared_r, 4096, NG, T)
        k_z = carve(shared_r, 6144, 2, G0, T)
        a_t = carve(shared_r, 2048, 2, T)
        v_nat = carve(v_mem, 0, NT, VW * H0 + ROWS - VW)
        v_heads = v_nat[:, :, 0:VW * H0].rearrange("p t (h d) -> p t h d", d=VW)
        xn = carve(v_mem, 0, NT, C)

        xn2 = carve(shared, 0, NT, C)
        x_tf = carve(shared, 512, T)
        x_gated = carve(shared, 1024, 2, T)
        silu = carve(shared, 2048, 2, FT, T)
        hidden = carve(shared, 4096, 2, FT, T)
        moe_t = carve(shared, 6144, T)
        scores_sb = carve(shared, 6656, NT, E)
        top = carve(shared, 6688, NT, E)
        top_at = carve(shared, 6720, NT, E)
        top_atf = carve(shared, 6752, NT, 2)
        chosen = carve(shared, 6784, 2, NT, E)
        gate_exp = carve(shared, 6848, NT, E)
        gate = carve(shared, 6880, NT, E)
        gates_nat = carve(shared, 6912, NT, 2 * E)
        xg_r = carve(shared_r, 0, 2, 2, T)
        h_r = carve(shared_r, 2048, 2, 2, FT, T)
        g_t = carve(shared_r, 6144, T)

        x_dup = carve(shared, 0, NT, 2, 2, D1)
        v1 = carve(shared, 1024, NT, KVH * D1)
        att = carve(shared, 2048, 3, CAUSAL)
        probs_t = carve(shared, 5888, 4, CAUSAL)
        wo_t = carve(shared, 0, T)
        xn4 = carve(shared, 512, NT, C)
        tok_r = carve(shared_r, 0, T)
        pos_r = carve(shared_r, 512, T)
        k_r = carve(shared_r, 1024, KVH, 2, T)
        q_r = carve(shared_r, 5120, 4, T)
        o_r = carve(shared_r, 7168, 2, 2, T)
        f_r = carve(shared_r, 4096, 2, T)

        psum = ctx.enter_context(nc.psum_tensor("psum", [P, 8, T], F32))

        def bank(i):
            return psum[:, i, :]

        def max_bank(n):
            return bank(4 + n % 3 if n < G0 * NT else 4 + (n + 1) % 2)

        def score_bank(i):
            at, col, _ = SCORE_AT[i]
            return bank(at)[:, col:col + P * (i + 1)]

        def whi(part, a, n):
            return w_hi[:, COL[part] + a:COL[part] + a + n]

        def wlo(part, a, n):
            return w_lo[:, COL[part] + a:COL[part] + a + n]

        weights_in = sem("weights_in")
        consts_in = sem("consts_in")
        ident_ready = sem("ident_ready")
        w_hi_ready = sem("w_hi_ready")
        w_lo_ready = sem("w_lo_ready")
        setup_pool = sem("setup_pool")
        x_loaded = sem("x_loaded")
        x_copied = sem("x_copied")
        pads_ready = sem("pads_ready")
        out_ready = sem("out_ready")
        out_stored = sem("out_stored")

        xn_ready = sem("xn_ready")
        xt_psum = sem("xt_psum")
        xt_hi_ready = sem("xt_hi_ready")
        xt_lo_ready = sem("xt_lo_ready")
        qkv_psum = sem("qkv_psum")
        qkv_ready = sem("qkv_ready")
        sq_ready = sem("sq_ready")
        v_ready = sem("v_ready")
        rms_ready = sem("rms_ready")
        k_normed = sem("k_normed")
        q_normed = sem("q_normed")
        k_hi_in = sem("k_hi_in")
        k_hi_twice = sem("k_hi_twice")
        k_lo_in = sem("k_lo_in")
        q_hi_in = sem("q_hi_in")
        q_lo_in = sem("q_lo_in")
        qt_first = sem("qt_first")
        kt_psum = sem("kt_psum")
        qt_psum = sem("qt_psum")
        kt_ready = sem("kt_ready")
        qt_ready = sem("qt_ready")
        zeroed = sem("zeroed")
        qz_ready = [sem(f"qz_ready_{j}") for j in range(G0)]
        kz_ready = [sem(f"kz_ready_{j}") for j in range(2)]
        s_psum = sem("s_psum")
        max_done = sem("max_done")
        max_in_q = sem("max_in_q")
        qm_psum = sem("qm_psum")
        qm_ready = sem("qm_ready")
        st_psum = sem("st_psum")
        exp_done = sem("exp_done")
        pv_done = sem("pv_done")
        o_copied = sem("o_copied")
        on_psum = sem("on_psum")
        on_ready = sem("on_ready")
        ot_psum = sem("ot_psum")
        ot_hi_ready = sem("ot_hi_ready")
        ot_lo_ready = sem("ot_lo_ready")
        proj_psum = sem("proj_psum")

        xn2_ready = sem("xn2_ready")
        xt2_psum = sem("xt2_psum")
        x_tf_ready = sem("x_tf_ready")
        score_psum = sem("score_psum")
        scores_copied = sem("scores_copied")
        gate_exp_ready = sem("gate_exp_ready")
        gates_ready = sem("gates_ready")
        gt_psum = sem("gt_psum")
        gt_ready = sem("gt_ready")
        gate_psum = sem("gate_psum")
        gated = sem("gated")
        xg_hi_ready = sem("xg_hi_ready")
        xg_lo_ready = sem("xg_lo_ready")
        mid_psum = sem("mid_psum")
        sw_psum = sem("sw_psum")
        silu_done = sem("silu_done")
        h_done = sem("h_done")
        h_hi_ready = sem("h_hi_ready")
        h_lo_dve = sem("h_lo_dve")
        h_lo_pool = sem("h_lo_pool")
        expert_psum = sem("expert_psum")
        moe_copied = sem("moe_copied")
        moe_psum = sem("moe_psum")

        x_dup_ready = sem("x_dup_ready")
        xd_psum = sem("xd_psum")
        xd_hi_ready = sem("xd_hi_ready")
        xd_lo_ready = sem("xd_lo_ready")
        k_psum = sem("k_psum")
        k_hi_ready = sem("k_hi_ready")
        k_lo_ready = sem("k_lo_ready")
        v_psum = sem("v_psum")
        v1_ready = sem("v1_ready")
        q_psum = sem("q_psum")
        q_hi_ready = sem("q_hi_ready")
        q_lo_ready = sem("q_lo_ready")
        s1_psum = sem("s1_psum")
        att_ready = sem("att_ready")
        exp1_done = sem("exp1_done")
        rden_ready = sem("rden_ready")
        p_ready = sem("p_ready")
        pt_psum = sem("pt_psum")
        pt_a_ready = sem("pt_a_ready")
        pt_b_ready = sem("pt_b_ready")
        pv1_done = sem("pv1_done")
        o_hi_ready = sem("o_hi_ready")
        o_lo_ready = sem("o_lo_ready")
        wo_psum = sem("wo_psum")
        wo_copied = sem("wo_copied")
        x3_psum = sem("x3_psum")
        xn4_ready = sem("xn4_ready")
        xt4_psum = sem("xt4_psum")
        f_hi_ready = sem("f_hi_ready")
        f_lo_ready = sem("f_lo_ready")
        ffn_psum = sem("ffn_psum")
        trig_in = sem("trig_in")
        trig_out = sem("trig_out")
        alibi_masked = sem("alibi_masked")
        queries_seen = sem("queries_seen")
        scores_seen = sem("scores_seen")
        rden_seen = sem("rden_seen")
        alibi_ready = sem("alibi_ready")
        rel_ready = sem("rel_ready")

        block = ctx.enter_context(nc.Block())

        @block.sync
        def _(sp):
            sp.dma_start(raw, w_all).then_inc(weights_in, 16)
            for dst, src in ((b_qkv_sb[:, :], b_qkv), (b_proj_sb[:, :], b_proj), (norm_w_raw[:, 0, :], qn_w),
                             (norm_w_raw[:, 1, :], kn_w)):
                sp.dma_start(dst, src.partition_broadcast(P)).then_inc(consts_in, 16)
            sp.dma_start(router_sb[:, :], router).then_inc(consts_in, 16)
            sp.dma_start(angle_sb[:, 0, :], angle.partition_broadcast(P)).then_inc(consts_in, 16)
            sp.dma_start(slope_sb[:, :], slopes.partition_broadcast(P)).then_inc(consts_in, 16)
            sp.sem_inc(out_stored, 16)
            sp.dma_start(x_in[:, :, :], x_dram[0]).then_inc(x_loaded, 16)

            def strips(b):
                def keys(g):
                    if g >= 2:
                        sp.wait_ge(st_psum, b * 32 + 8 * (g - 1))
                    for j in range(G0):
                        rows = slice(ROWS * j, ROWS * j + ROWS)
                        sp.dma_start(k_z[rows, g % 2, j, :].bitcast(F32), k_t[rows, g, :].bitcast(F32)).then_inc(kz_ready[g % 2], 16)

                def queries(h):
                    g, j = h // G0, h % G0
                    rows = slice(ROWS * j, ROWS * j + ROWS)
                    if g > 1:
                        sp.wait_ge(s_psum, b * H0 * NT + NT * (h - G0 + 1))
                    sp.dma_start(q_z[rows, j, :].bitcast(F32), q_t[rows, g, :].bitcast(F32)).then_inc(qz_ready[j], 16)

                sp.wait_ge(zeroed, b + 1)
                sp.wait_ge(qt_ready, b * (NG - 1) + 1)
                queries(G0)
                sp.wait_ge(kt_ready, b * NG + 1)
                keys(0)
                sp.wait_ge(kt_ready, b * NG + NG)
                for h in range(G0 + 1, H0):
                    queries(h)
                    if h == 2 * G0:
                        keys(1)
                    if h == 12:
                        keys(2)
                keys(3)

            if NB > 1:
                with sp.Fori(0, NB - 1) as b:
                    sp.wait_ge(xn_ready, b + 1)
                    sp.wait_ge(x_copied, b + 1)
                    sp.dma_start(x_in[:, :, :], x_dram[b + 1]).then_inc(x_loaded, 16)
                    strips(b)
                    sp.wait_ge(out_ready, b + 1)
                    sp.dma_start(out_dram[b], x_res[:, :, :]).then_inc(out_stored, 16)
            sp.wait_ge(xn_ready, NB)
            sp.wait_ge(x_copied, NB)
            sp.dma_start(x_in[:, :, :], x_dram[NB - 1]).then_inc(x_loaded, 16)
            strips(NB - 1)
            sp.wait_ge(out_ready, NB)
            sp.dma_start(out_dram[NB - 1], x_res[:, :, :]).then_inc(out_stored, 16)
            sp.wait_ge(out_stored, 16 * NB + 16)

        @block.gpsimd
        def _(pool):
            pool.memset(ident[:, :], 0.0)
            pool.drain()
            pool.affine_select(out=ident[:, :], in_=ident[:, :], compare_op=ALU.not_equal, fill=1.0, base=0,
                               pattern=[[-1, P]], channel_multiplier=1)
            pool.iota(expert_ids[:, :], pattern=[[1, E]], base=0, channel_multiplier=0,
                      allow_small_or_imprecise_dtypes=True)
            pool.drain()
            pool.tensor_tensor(pick[:, :], ident[0:2 * E, 0:E], ident[0:2 * E, E:2 * E], ALU.add).then_inc(ident_ready, 1)
            pool.iota(x_res[:, :, :].rearrange("p t c -> p (t c)"), pattern=[[-1, T]], base=T - P,
                      channel_multiplier=1, allow_small_or_imprecise_dtypes=True).then_inc(rel_ready, 1)
            pool.wait_ge(alibi_ready, 1)
            pool.affine_select(out=alibi[:, :, T - P:T], in_=alibi[:, :, T - P:T], compare_op=ALU.is_ge, fill=-BIG,
                               base=0, pattern=[[0, H1], [-1, P]],
                               channel_multiplier=1).then_inc(alibi_masked, 1)
            with pool.Fori(0, NB) as b:
                pool.wait_ge(rms_ready, b + 1)
                for t in range(NT):
                    m = pool.tensor_tensor(qk_w[:, t, C:QK].rearrange("p (h d) -> p h d", d=D0),
                                           qkv[:, t, C:QK].rearrange("p (h d) -> p h d", d=D0),
                                           ms_y[:, t, H0:2 * H0][:, :, None].broadcast_to([P, H0, D0]), ALU.mult)
                m.then_inc(k_normed, 1)
                pool.memset(nat_k[:, :, :, AUG + 2:ROWS], 0.0)
                pool.memset(nat_k[:, :, :, AUG:AUG + 2], 1.0)
                for t in range(NT):
                    pool.tensor_copy(v_heads[:, t, :, 0:D0],
                                     qkv[:, t, QK:3 * C].rearrange("p (h d) -> p h d", d=D0))
                pool.memset(v_heads[:, :, :, D0:VW], 1.0)
                pool.memset(v_nat[:, :, VW * H0:VW * H0 + ROWS - VW], 0.0).then_inc(v_ready, 1)
                pool.wait_ge(q_normed, b + 1)
                pool.sem_inc(queries_seen, 1)
                pool.memset(nat_q[:, :, :, AUG:ROWS], 0.0).then_inc(pads_ready, 1)
                pool.wait_ge(out_stored, b * 16 + 16)
                for t in range(NT):
                    m = pool.tensor_tensor(x_res[:, t, :], x_in[:, t, :], b_proj_sb[:, :], ALU.add)
                m.then_inc(x_copied, 1)
                pool.memset(q_z.bitcast(F32), 0.0)
                pool.memset(k_z.bitcast(F32), 0.0).then_inc(zeroed, 1)

                for k in range(NE):
                    pool.wait_ge(xg_hi_ready, b * NE + k + 1)
                    pool.tensor_tensor(xg_r[:, k % 2, 1, :], x_gated[:, k % 2, :] if k else x_tf,
                                       xg_r[:, k % 2, 0, :].bitcast(F32), ALU.subtract).then_inc(xg_lo_ready, 1)
                    if k > 0:
                        j = k - 1
                        pool.wait_ge(h_hi_ready, b * NE + j + 1)
                        pool.tensor_tensor(h_r[:, j % 2, 1, 1, :], hidden[:, j % 2, 1, :],
                                           h_r[:, j % 2, 0, 1, :].bitcast(F32), ALU.subtract).then_inc(h_lo_pool, 1)
                j = NE - 1
                pool.wait_ge(h_hi_ready, b * NE + j + 1)
                pool.tensor_tensor(h_r[:, j % 2, 1, 1, :], hidden[:, j % 2, 1, :],
                                   h_r[:, j % 2, 0, 1, :].bitcast(F32), ALU.subtract).then_inc(h_lo_pool, 1)

                for h in range(H1):
                    pool.wait_ge(rden_ready, b * H1 + h + 1)
                    pool.sem_inc(rden_seen, 1)
                    for i in TILES:
                        p = att[:, h % 3, ROW_AT[i]:ROW_AT[i] + P * (i + 1)]
                        pool.tensor_scalar(p, p, rden[:, h, i:i + 1], 1.0, ALU.mult, ALU.mult).then_inc(p_ready, 1)

        @block.scalar
        def _(act):
            act.wait_ge(weights_in, 16)
            act.wait_ge(consts_in, 16 * 7)
            act.activation(slope_sb[:, :], slope_sb[:, :], ACT.Exp).then_inc(trig_out, 1)
            act.wait_ge(trig_in, 1)
            act.activation(angle_sb[:, 2, :], angle_sb[:, 1, :], ACT.Sin)
            act.activation(angle_sb[:, 3, :], angle_sb[:, 1, :], ACT.Sin, scale=0.5).then_inc(trig_out, 1)
            act.wait_ge(trig_in, 2)
            act.activation(raw[:, COL["sign"]:COL["sign"] + C], raw[:, COL["sign"]:COL["sign"] + C], ACT.Sign)
            act.drain()
            act.activation(w_hi[:, :], raw, ACT.Copy).then_inc(w_hi_ready, 1)

            def start_x(b, ahead):
                act.wait_ge(xt_psum, b + ahead + 1)
                act.activation(x_t[:, 0, :], bank(0), ACT.Copy).then_inc(xt_hi_ready, 1)

            def start_squares(b, ahead):
                for t in range(NT):
                    act.wait_ge(qkv_ready, b * NT + ahead * NT + t + 1)
                    act.activation(qk_sq[:, t, :], qkv[:, t, 0:QK], ACT.Square).then_inc(sq_ready, 1)

            start_x(0, 0)
            start_squares(0, 0)
            with act.Fori(0, NB) as b:
                qv = qk_w[:, :, 0:C].rearrange("p t (h d) -> p t h d", d=D0)
                kv = qk_w[:, :, C:QK].rearrange("p t (h d) -> p t h d", d=D0)
                act.wait_ge(k_normed, b + 1)
                act.activation(nat_k[:, :, :, 0:D0].bitcast(F32R), kv, ACT.Copy).then_inc(k_hi_in, 1)
                act.activation(nat_k[:, :, :, 2 * D0:3 * D0].bitcast(F32R), kv, ACT.Copy).then_inc(k_hi_twice, 1)
                act.wait_ge(q_normed, b + 1)
                act.activation(nat_q[:, :, :, 0:D0].bitcast(F32R), qv, ACT.Copy).then_inc(q_hi_in, 1)
                for g in range(NG):
                    act.wait_ge(kt_psum, b * NG + g + 1)
                    act.activation(k_t[:, g, :], bank(g), ACT.Copy).then_inc(kt_ready, 1)
                    if g + 1 < NG:
                        act.wait_ge(qt_psum, b * NG + g + 2)
                        act.activation(q_t[:, g + 1, :], bank(5 + g), ACT.Copy).then_inc(qt_ready, 1)

                def copy_qm(g):
                    act.wait_ge(qm_psum, b * NG + g + 1)
                    act.activation(q_t[:, g, :], bank(7), ACT.Copy).then_inc(qm_ready, 1)

                def copy_o(g):
                    act.wait_ge(pv_done, b * 4 * NG + 4 * g + 4)
                    act.activation(o_t, bank(6), ACT.Copy).then_inc(o_copied, 1)

                act.wait_ge(v_ready, b + 1)
                copy_qm(0)
                for g in range(NG):
                    for kb in range(NT):
                        q = g * NT + kb
                        if q >= 2:
                            act.wait_ge(pv_done, b * 4 * NG + q - 1)
                        for half in range(2):
                            if half and kb == NT - 1 and g + 1 < NG:
                                copy_qm(g + 1)
                            n = 2 * q + half
                            act.wait_ge(st_psum, b * 32 + n + 1)
                            act.activation(probs[:, q % 2, 2 * half:2 * half + 2, :],
                                           psum[:, 2 * half:2 * half + 2, :], ACT.Exp).then_inc(exp_done, 1)
                        if kb == 0 and g > 0:
                            copy_o(g - 1)
                copy_o(NG - 1)
                act.wait_ge(ot_psum, b + 1)
                act.activation(a_t[:, 0, :], bank(0), ACT.Copy).then_inc(ot_hi_ready, 1)

                act.wait_ge(xt2_psum, b + 1)
                act.activation(x_tf, bank(0), ACT.Copy).then_inc(x_tf_ready, 1)
                act.activation(xg_r[:, 0, 0, :], bank(0), ACT.Copy).then_inc(xg_hi_ready, 1)
                act.wait_ge(scores_copied, b + 1)
                act.activation(gate_exp, scores_sb, ACT.Exp, scale=-1.0).then_inc(gate_exp_ready, 1)

                def silu_of(k):
                    act.wait_ge(mid_psum, b * NE + k + 1)
                    if k >= 2:
                        act.wait_ge(h_done, b * NE + k - 1)
                    act.activation(silu[:, k % 2, :, :], psum[:, 2:4, :], ACT.Silu).then_inc(silu_done, 1)

                for k in range(NE):
                    silu_of(k)
                    if k == 0:
                        act.wait_ge(gt_psum, b + 1)
                        act.activation(g_t[0:2 * E, :], bank(1)[0:2 * E, :], ACT.Copy).then_inc(gt_ready, 1)
                    if k + 1 < NE:
                        act.wait_ge(gated, b * E + k + 1)
                        if k >= 1:
                            act.wait_ge(sw_psum, b * NE + k)
                        act.activation(xg_r[:, (k + 1) % 2, 0, :], x_gated[:, (k + 1) % 2, :],
                                       ACT.Copy).then_inc(xg_hi_ready, 1)
                    act.wait_ge(h_done, b * NE + k + 1)
                    if k >= 2:
                        act.wait_ge(expert_psum, b * NE + k - 1)
                    act.activation(h_r[:, k % 2, 0, :, :], hidden[:, k % 2, :, :], ACT.Copy).then_inc(h_hi_ready, 1)
                act.wait_ge(expert_psum, b * NE + NE)
                act.activation(moe_t, bank(6), ACT.Copy).then_inc(moe_copied, 1)

                for j, dst in enumerate((tok_r, pos_r)):
                    act.wait_ge(xd_psum, b * 2 + j + 1)
                    act.activation(dst, bank(j), ACT.Copy).then_inc(xd_hi_ready, 1)

                def q_hi(h):
                    half = D1 * (h % 2)
                    act.wait_ge(q_psum, b * (H1 // 2) + h // 2 + 1)
                    act.activation(q_r[0:D1, h % 4, :], bank(0)[half:half + D1, :], ACT.Copy).then_inc(q_hi_ready, 1)

                def k_hi(g):
                    act.wait_ge(k_psum, b * KVH + g + 1)
                    act.activation(k_r[:, g, 0, :], bank(2 + g), ACT.Copy).then_inc(k_hi_ready, 1)

                k_hi(0)
                q_hi(0)
                q_hi(1)
                for g in range(1, KVH):
                    k_hi(g)
                for j in range(2):
                    act.wait_ge(v_psum, b * 2 + j + 1)
                    act.activation(v1[:, 2 * j:2 * j + 2, :], bank(6 + j), ACT.Copy).then_inc(v1_ready, 1)
                for s in range(H1 + 4):
                    if s + 2 < H1:
                        q_hi(s + 2)
                    if s < H1:
                        for n, i in enumerate(TILES):
                            a = att[:, s % 3, ROW_AT[i]:ROW_AT[i] + P * (i + 1)]
                            act.wait_ge(att_ready, b * 4 * H1 + 4 * s + n + 1)
                            act.activation(a, a, ACT.Exp, bias=neg_m[:, s, i:i + 1], scale=-1.0,
                                           accum_out=sums[:, s, i:i + 1]).then_inc(exp1_done, 1)
                    if s % 2 == 1 and s >= 5:
                        p = (s - 5) // 2
                        act.wait_ge(pv1_done, b * (H1 // 2) + p + 1)
                        if p >= 2:
                            act.wait_ge(wo_psum, b * (H1 // 2) + p - 1)
                        act.activation(o_r[:, p % 2, 0, :], bank(6), ACT.Copy).then_inc(o_hi_ready, 1)
                    h = s - 2
                    if 0 <= h < H1:
                        act.wait_ge(pt_psum, b * H1 + h + 1)
                        if h >= 4:
                            act.wait_ge(pv1_done, b * (H1 // 2) + (h - 4) // 2 + 1)
                        act.activation(probs_t[:, h % 4, 0:2 * T],
                                       psum[:, 3:5, :].rearrange("p a c -> p (a c)"), ACT.Copy).then_inc(pt_a_ready, 1)
                start_x(b, 1)
                act.wait_ge(wo_psum, b * (H1 // 2) + H1 // 2)
                act.activation(wo_t, bank(7), ACT.Copy).then_inc(wo_copied, 1)
                start_squares(b, 1)
                act.wait_ge(xt4_psum, b + 1)
                act.activation(f_r[:, 0, :], bank(6), ACT.Copy).then_inc(f_hi_ready, 1)

        @block.vector
        def _(dve):
            def rsqrt_guess(y, half):
                dve.tensor_scalar(y.bitcast(I32), half.bitcast(I32), -0.5,
                                  float(0x5F3759DF - 2 ** 22 - 2 ** 30), ALU.mult, ALU.add)

            def rsqrt_step(y, half, tmp):
                dve.tensor_tensor(tmp, y, y, ALU.mult)
                dve.drain()
                dve.tensor_tensor(tmp, tmp, half, ALU.mult)
                dve.drain()
                return dve.scalar_tensor_tensor(y, tmp, 1.5, y, ALU.add, ALU.mult)

            def rsqrt(y, half, tmp):
                rsqrt_guess(y, half)
                dve.drain()
                rsqrt_step(y, half, tmp)
                dve.drain()
                rsqrt_step(y, half, tmp)
                dve.drain()
                return rsqrt_step(y, half, tmp)

            def layernorm_stats(src):
                for t in range(NT):
                    dve.bn_stats(stats[:, t, :], src[:, t, :])
                dve.drain()
                for t in range(NT):
                    dve.bn_aggr(mean_var[:, t, :], stats[:, t, :])
                dve.drain()
                dve.tensor_scalar(half_var[:, :], mean_var[:, :, 1], -0.5, -0.5 * LN_EPS, ALU.mult, ALU.add)
                dve.drain()
                rsqrt(rstd[:, :], half_var[:, :], stats[:, :, 0])
                dve.drain()

            def normalise_x(src, dst):
                layernorm_stats(src)
                for t in range(NT):
                    m = dve.tensor_scalar(dst[:, t, :], src[:, t, :], mean_var[:, t, 0:1], rstd[:, t:t + 1],
                                          ALU.subtract, ALU.mult)
                return m

            def start_x(b, ahead):
                dve.wait_ge(xt_hi_ready, b + ahead + 1)
                dve.tensor_tensor(x_t[:, 1, :], bank(0), x_t[:, 0, :].bitcast(F32),
                                  ALU.subtract).then_inc(xt_lo_ready, 1)

            def start_qkv(b, ahead):
                for t in range(NT):
                    dve.wait_ge(qkv_psum, b * NT + ahead * NT + t + 1)
                    dve.tensor_tensor(qkv[:, t, :], bank(1 + t)[:, 0:3 * C], b_qkv_sb[:, :],
                                      ALU.add).then_inc(qkv_ready, 1)

            def start_rms(b, ahead):
                dve.wait_ge(sq_ready, b * NT + ahead * NT + NT)
                dve.tensor_reduce(ms, qk_sq.rearrange("p t (h d) -> p (t h) d", d=D0), AX.X, ALU.add)
                dve.drain()
                dve.tensor_scalar(ms, ms, -0.5 / D0, -0.5 * RMS_EPS, ALU.mult, ALU.add)
                if ahead:
                    for t in range(NT):
                        dve.bn_aggr(mean_var[:, t, :], stats[:, t, :])
                    dve.drain()
                    dve.tensor_scalar(root_half[:, 0:NT], mean_var[:, :, 1], -0.5, -0.5 * LN_EPS, ALU.mult, ALU.add)
                dve.drain()
                which = slice(0 if ahead else NT, NT + NT * 2 * H0)
                rsqrt(root_y[:, which], root_half[:, which], root_tmp[:, which]).then_inc(rms_ready, 1)
                dve.drain()

            def start_queries(b, ahead):
                queries = qkv[:, :, 0:C].rearrange("p t (h d) -> p t h d", d=D0)
                qv = qk_w[:, :, 0:C].rearrange("p t (h d) -> p t h d", d=D0)
                dve.tensor_tensor(qv, queries, ms_y[:, :, 0:H0][:, :, :, None].broadcast_to([P, NT, H0, D0]), ALU.mult)
                dve.drain()
                dve.tensor_tensor(qv, qv, q_weight[:, :, :][:, None, :, :].broadcast_to([P, NT, H0, D0]),
                                  ALU.mult).then_inc(q_normed, 1)

            def dve_l1(b):
                dve.drain()
                layernorm_stats(x_res)
                for t in range(NT):
                    m = dve.tensor_scalar(x_dup[:, t, :, :, :],
                                          x_res[:, t, :].rearrange("p (a c) -> p a c", a=2)[:, :, None, :].broadcast_to([P, 2, 2, D1]),
                                          mean_var[:, t, 0:1], rstd[:, t:t + 1], ALU.subtract, ALU.mult)
                m.then_inc(x_dup_ready, 1)
                low = slice(D1, P)
                for j, dst in enumerate((tok_r, pos_r)):
                    dve.wait_ge(xd_hi_ready, b * 2 + j + 1)
                    dve.tensor_tensor(dst[low, :], bank(j)[low, :], dst[low, :].bitcast(F32),
                                      ALU.subtract).then_inc(xd_lo_ready, 1)
                def k_lo(g):
                    dve.wait_ge(k_hi_ready, b * KVH + g + 1)
                    dve.tensor_tensor(k_r[:, g, 1, :], bank(2 + g), k_r[:, g, 0, :].bitcast(F32),
                                      ALU.subtract).then_inc(k_lo_ready, 1)

                def q_lo(h):
                    half = D1 * (h % 2)
                    dve.wait_ge(q_hi_ready, b * H1 + h + 1)
                    dve.tensor_tensor(q_r[low, h % 4, :], bank(0)[half:half + D1, :],
                                      q_r[0:D1, h % 4, :].bitcast(F32), ALU.subtract).then_inc(q_lo_ready, 1)

                def ahead(s):
                    y, half, tmp = rstd[:, :], half_var[:, :], stats[:, :, 0]
                    n = s - LN_AT
                    if n < 0 or n > 7:
                        return
                    dve.drain()
                    if n == 0:
                        dve.wait_ge(x_loaded, b * 16 + 32)
                        for t in range(NT):
                            dve.bn_stats(stats[:, t, :], x_in[:, t, :])
                    elif n == 1:
                        for t in range(NT):
                            dve.bn_aggr(mean_var[:, t, :], stats[:, t, :])
                    elif n == 2:
                        dve.tensor_scalar(half, mean_var[:, :, 1], -0.5, -0.5 * LN_EPS, ALU.mult, ALU.add)
                    elif n == 3:
                        rsqrt_guess(y, half)
                    elif n < 7:
                        rsqrt_step(y, half, tmp)
                    else:
                        for t in range(NT):
                            m = dve.tensor_scalar(xn[:, t, :], x_in[:, t, :], mean_var[:, t, 0:1], rstd[:, t:t + 1],
                                                  ALU.subtract, ALU.mult)
                        m.then_inc(xn_ready, 1)

                k_lo(0)
                q_lo(0)
                q_lo(1)
                for g in range(1, KVH):
                    k_lo(g)
                for s in range(H1 + 4):
                    h = s - 1
                    if 0 <= h < H1:
                        dve.wait_ge(exp1_done, b * 4 * H1 + 4 * h + 4)
                        dve.tensor_scalar(sums[:, h, :], sums[:, h, :], 1.0, None, ALU.add)
                        dve.drain()
                        dve.reciprocal(rden[:, h, :], sums[:, h, :]).then_inc(rden_ready, 1)
                    if s < H1:
                        for n, i in enumerate(TILES):
                            if n != 2:
                                dve.wait_ge(s1_psum, b * 3 * H1 + 3 * s + (1, 2, 2, 3)[n])
                                dve.sem_inc(scores_seen, 1)
                            dve.tensor_tensor_reduce(att[:, s % 3, ROW_AT[i]:ROW_AT[i] + P * (i + 1)], score_bank(i),
                                                     alibi[:, s, T - P * (i + 1):T], -1.0, BIG, ALU.add, ALU.min,
                                                     neg_m[:, s, i:i + 1]).then_inc(att_ready, 1)
                    if s + 2 < H1:
                        q_lo(s + 2)
                    ahead(s)
                    h = s - 2
                    if 0 <= h < H1:
                        dve.wait_ge(pt_psum, b * H1 + h + 1)
                        if h >= 4:
                            dve.wait_ge(pv1_done, b * (H1 // 2) + (h - 4) // 2 + 1)
                        dve.tensor_copy(probs_t[:, h % 4, 2 * T:CAUSAL], bank(5)[:, 0:CAUSAL - 2 * T]).then_inc(pt_b_ready, 1)
                    if s % 2 == 1 and s >= 5:
                        p = (s - 5) // 2
                        dve.wait_ge(o_hi_ready, b * (H1 // 2) + p + 1)
                        dve.tensor_tensor(o_r[:, p % 2, 1, :], bank(6), o_r[:, p % 2, 0, :].bitcast(F32),
                                          ALU.subtract).then_inc(o_lo_ready, 1)
                start_x(b, 1)
                start_qkv(b, 1)
                dve.wait_ge(x3_psum, b + 1)
                flat = x_res[:, :, :].rearrange("p t c -> p (t c)")
                dve.tensor_tensor(flat, bank(5), flat, ALU.add)
                dve.drain()
                for t in range(NT):
                    dve.bn_stats(stats[:, t, :], x_res[:, t, :])
                start_rms(b, 1)
                for t in range(NT):
                    m = dve.tensor_scalar(xn4[:, t, :], x_res[:, t, :], mean_var[:, t, 0:1], root_y[:, t:t + 1],
                                          ALU.subtract, ALU.mult)
                m.then_inc(xn4_ready, 1)
                dve.wait_ge(f_hi_ready, b + 1)
                dve.tensor_tensor(f_r[:, 1, :], bank(6), f_r[:, 0, :].bitcast(F32), ALU.subtract).then_inc(f_lo_ready, 1)
                start_queries(b, 1)
                dve.wait_ge(ffn_psum, b + 1)
                dve.tensor_tensor(flat, bank(7), flat, ALU.add).then_inc(out_ready, 1)
                dve.drain()

            def dve_moe(b):
                dve.drain()
                normalise_x(x_res, xn2).then_inc(xn2_ready, 1)
                dve.wait_ge(score_psum, b + 1)
                dve.tensor_copy(scores_sb, bank(1)[:, 0:NT * E].rearrange("p (t e) -> p t e", e=E)).then_inc(scores_copied, 1)
                dve.drain()
                for t in range(NT):
                    dve.max(top[:, t, :], scores_sb[:, t, :])
                dve.drain()
                for t in range(NT):
                    dve.max_index(top_at[:, t, :].bitcast(U32), top[:, t, :], scores_sb[:, t, :])
                dve.drain()
                dve.tensor_copy(top_atf, top_at[:, :, 0:2].bitcast(U32))
                dve.drain()
                for j in range(2):
                    dve.tensor_tensor(chosen[:, j, :, :], expert_ids[:, None, :].broadcast_to([P, NT, E]),
                                      top_atf[:, :, j:j + 1].broadcast_to([P, NT, E]), ALU.is_equal)
                dve.wait_ge(gate_exp_ready, b + 1)
                dve.tensor_scalar(gate_exp, gate_exp, 1.0, None, ALU.add)
                dve.drain()
                dve.reciprocal(gate, gate_exp)
                dve.tensor_tensor(chosen[:, 0, :, :], chosen[:, 0, :, :], chosen[:, 1, :, :], ALU.add)
                dve.drain()
                dve.tensor_tensor(gate, gate, chosen[:, 0, :, :], ALU.mult)
                dve.drain()
                dve.tensor_copy(gates_nat[:, :, 0:E].bitcast(F32R), gate)
                dve.drain()
                dve.tensor_tensor(gates_nat[:, :, E:2 * E], gate, gates_nat[:, :, 0:E], ALU.subtract).then_inc(gates_ready, 1)

                def gate_x(k):
                    dve.wait_ge(gate_psum, b * E + k)
                    if k >= 3:
                        dve.wait_ge(xg_lo_ready, b * NE + k - 1)
                    dve.tensor_tensor(x_gated[:, k % 2, :], bank(7), x_tf, ALU.mult).then_inc(gated, 1)

                gate_x(1)
                for k in range(NE):
                    dve.wait_ge(sw_psum, b * NE + k + 1)
                    dve.wait_ge(silu_done, b * NE + k + 1)
                    if k >= 2:
                        dve.wait_ge(h_lo_pool, b * NE + k - 1)
                    dve.tensor_tensor(hidden[:, k % 2, :, :], psum[:, 4:6, :], silu[:, k % 2, :, :],
                                      ALU.mult).then_inc(h_done, 1)
                    if 1 <= k + 2 < NE:
                        gate_x(k + 2)
                    dve.wait_ge(h_hi_ready, b * NE + k + 1)
                    dve.tensor_tensor(h_r[:, k % 2, 1, 0, :], hidden[:, k % 2, 0, :],
                                      h_r[:, k % 2, 0, 0, :].bitcast(F32), ALU.subtract).then_inc(h_lo_dve, 1)
                dve.wait_ge(moe_psum, b + 1)
                dve.tensor_tensor(x_res[:, :, :].rearrange("p t c -> p (t c)"), bank(0),
                                  x_res[:, :, :].rearrange("p t c -> p (t c)"), ALU.add)
                dve_l1(b)
            dve.wait_ge(consts_in, 16 * 7)
            norm_w = alibi[:, 2, 0:2 * C].rearrange("p (a h d) -> p a h d", a=2, h=H0)
            dve.tensor_copy(norm_w, norm_w_raw[:, :, None, :].broadcast_to([P, 2, H0, D0]))
            dve.drain()
            dve.scalar_tensor_tensor(q_weight[:, :, :], norm_w[:, 0], D0 ** -0.5, norm_w[:, 1], ALU.mult, ALU.mult)
            scratch = alibi[:, 0:2, :].rearrange("p a c -> p (a c)")
            turns = scratch[:, 0:H1]
            dve.tensor_scalar(turns, angle_sb[:, 0, :], 1.0 / (2 * math.pi), None, ALU.mult)
            dve.drain()
            dve.tensor_copy(scratch[:, 64:64 + H1].bitcast(I32), turns)
            dve.drain()
            dve.tensor_copy(turns, scratch[:, 64:64 + H1].bitcast(I32))
            dve.drain()
            for part in TURN:
                dve.tensor_scalar(scratch[:, 128:128 + H1], turns, -part, None, ALU.mult)
                dve.drain()
                dve.tensor_tensor(angle_sb[:, 0, :], angle_sb[:, 0, :], scratch[:, 128:128 + H1], ALU.add)
                dve.drain()
            dve.tensor_scalar(angle_sb[:, 1, :], angle_sb[:, 0, :], PI_DOWN, -PI_DOWN, ALU.min, ALU.max).then_inc(trig_in, 1)
            dve.wait_ge(trig_out, 2)
            dve.tensor_tensor(angle_sb[:, 3, :], angle_sb[:, 3, :], angle_sb[:, 3, :], ALU.mult)
            dve.drain()
            dve.tensor_scalar(angle_sb[:, 3, :], angle_sb[:, 3, :], -2 * D1 ** -0.5, D1 ** -0.5, ALU.mult, ALU.add)
            dve.tensor_scalar(angle_sb[:, 2, :], angle_sb[:, 2, :], D1 ** -0.5, None, ALU.mult)
            dve.drain()
            dve.wait_ge(weights_in, 16)
            pairs = raw[:, COL["wq"]:COL["wq"] + H1 * D1].rearrange("p (h d two) -> p two h d", h=H1, two=2)
            sin_a = angle_sb[:, 2, :][:, :, None].broadcast_to([P, H1, D1 // 2])
            cos_a = angle_sb[:, 3, :][:, :, None].broadcast_to([P, H1, D1 // 2])
            terms = [alibi[:, 4 + j, :].rearrange("p (h d) -> p h d", h=H1) for j in range(4)]
            for term, side, turn in zip(terms, (0, 1, 0, 1), (cos_a, sin_a, sin_a, cos_a)):
                dve.tensor_tensor(term, pairs[:, side], turn, ALU.mult)
            dve.drain()
            dve.tensor_tensor(pairs[:, 0], terms[0], terms[1], ALU.subtract)
            dve.tensor_tensor(pairs[:, 1], terms[2], terms[3], ALU.add).then_inc(trig_in, 1)
            dve.drain()
            dve.wait_ge(rel_ready, 1)
            dve.wait_ge(trig_out, 2)
            for h in range(H1):
                m = dve.tensor_scalar(alibi[:, h, :], x_res[:, :, :].rearrange("p t c -> p (t c)"),
                                      slope_sb[:, h:h + 1], None, ALU.mult)
            m.then_inc(alibi_ready, 1)
            dve.wait_ge(w_hi_ready, 1)
            dve.tensor_tensor(w_lo[:, :], raw, w_hi[:, :].bitcast(F32), ALU.subtract).then_inc(w_lo_ready, 1)
            dve.drain()
            dve.wait_ge(alibi_masked, 1)
            dve.wait_ge(x_loaded, 16)
            normalise_x(x_in, xn).then_inc(xn_ready, 1)
            dve.drain()
            start_x(0, 0)
            start_qkv(0, 0)
            start_rms(0, 0)
            start_queries(0, 0)
            dve.drain()
            with dve.Fori(0, NB) as b:
                qv = qk_w[:, :, 0:C].rearrange("p t (h d) -> p t h d", d=D0)
                kv = qk_w[:, :, C:QK].rearrange("p t (h d) -> p t h d", d=D0)
                dve.wait_ge(k_hi_in, b + 1)
                dve.tensor_tensor(nat_k[:, :, :, D0:2 * D0], kv, nat_k[:, :, :, 0:D0],
                                  ALU.subtract).then_inc(k_lo_in, 1)
                dve.drain()
                dve.tensor_copy(nat_q[:, :, :, D0:2 * D0].bitcast(F32R), qv)
                dve.wait_ge(q_hi_in, b + 1)
                dve.tensor_tensor(nat_q[:, :, :, 2 * D0:3 * D0], qv, nat_q[:, :, :, 0:D0],
                                  ALU.subtract).then_inc(q_lo_in, 1)
                dve.wait_ge(qt_psum, b * NG + 1)
                dve.tensor_copy(q_t[:, 0, :], bank(4)).then_inc(qt_first, 1)

                def head_max(h):
                    for i in range(NT):
                        n = h * NT + i
                        dve.wait_ge(s_psum, b * 64 + n + 1)
                        dve.tensor_reduce(neg_max[:, i, h:h + 1], max_bank(n), AX.X, ALU.max,
                                          negate=True).then_inc(max_done, 1)

                def split_max(g):
                    hs = slice(G0 * g, G0 * g + G0)
                    dve.drain()
                    dve.tensor_copy(nat_q[:, :, hs, AUG].bitcast(F32R), neg_max[:, :, hs])
                    dve.drain()
                    dve.tensor_tensor(nat_q[:, :, hs, AUG + 1], neg_max[:, :, hs], nat_q[:, :, hs, AUG],
                                      ALU.subtract).then_inc(max_in_q, 1)

                def normalise(g):
                    ob = bank(7).rearrange("p (t r d) -> p t r d", t=NT, r=G0)
                    dve.wait_ge(on_psum, b * NG + g + 1)
                    dve.reciprocal(rec, ob[:, :, :, D0])
                    dve.drain()
                    dve.tensor_tensor(o_nat[:, :, G0 * D0 * g:G0 * D0 * (g + 1)].rearrange("p t (r d) -> p t r d", r=G0),
                                      ob[:, :, :, 0:D0], rec[:, :, :, None].broadcast_to([P, NT, G0, D0]),
                                      ALU.mult).then_inc(on_ready, 1)

                for h in range(LEAD):
                    head_max(h)
                    if h % G0 == G0 - 1:
                        split_max(h // G0)
                for q in range(H0):
                    if q + LEAD < H0:
                        head_max(q + LEAD)
                        if (q + LEAD) % G0 == G0 - 1:
                            split_max((q + LEAD) // G0)
                    if q % NT == 1 and q > NT:
                        normalise(q // NT - 1)
                normalise(NG - 1)
                dve.wait_ge(ot_hi_ready, b + 1)
                dve.tensor_tensor(a_t[:, 1, :], bank(0), a_t[:, 0, :].bitcast(F32),
                                  ALU.subtract).then_inc(ot_lo_ready, 1)
                dve.wait_ge(proj_psum, b + 1)
                dve.wait_ge(x_copied, b + 1)
                dve.tensor_tensor(x_res[:, :, :].rearrange("p t c -> p (t c)"), bank(1),
                                  x_res[:, :, :].rearrange("p t c -> p (t c)"), ALU.add)
                dve_moe(b)

        @block.tensor
        def _(pe):
            def transposes(to, tiles):
                for t, tile in enumerate(tiles):
                    m = pe.transpose(to[:, P * t:P * t + P], tile, ident[:, :])
                return m

            def product(to, left, right, start=True, stop=True):
                (lh, ll), (rh, rl) = left, right
                pe.matmul(to, lh, rh, start=start, stop=False)
                pe.matmul(to, lh, rl, start=False, stop=False)
                return pe.matmul(to, ll, rh, start=False, stop=stop)

            def start_x(b, ahead):
                pe.wait_ge(xn_ready, b + ahead + 1)
                transposes(bank(0), [xn[:, t, :] for t in range(NT)]).then_inc(xt_psum, 1)

            def start_qkv(b, ahead):
                pe.wait_ge(xt_lo_ready, b + ahead + 1)
                for t in range(NT):
                    ts = slice(P * t, P * t + P)
                    product(bank(1 + t)[:, 0:3 * C], (x_t[:, 0, ts], x_t[:, 1, ts]),
                            (whi("qkv", 0, 3 * C), wlo("qkv", 0, 3 * C))).then_inc(qkv_psum, 1)

            def pe_l1(b):
                pe.wait_ge(x_dup_ready, b + 1)
                for j in range(2):
                    transposes(bank(j), [x_dup[:, t, j, :, :] for t in range(NT)]).then_inc(xd_psum, 1)

                def head(part, n, to):
                    pe.matmul(to, whi(part, P * n, P), pos_r, start=True, stop=False)
                    return pe.matmul(to, wlo(part, P * n, P), pos_r, start=False, stop=True)

                pe.wait_ge(xd_lo_ready, b * 2 + 2)

                def queries(p):
                    if p > 0:
                        pe.wait_ge(q_lo_ready, b * H1 + 2 * p)
                    head("wq", p, bank(0)).then_inc(q_psum, 1)

                def scores1(h, i):
                    if i == TILES[0]:
                        pe.wait_ge(q_lo_ready, b * H1 + h + 1)
                        if h % REP == 0:
                            pe.wait_ge(k_lo_ready, b * KVH + h // REP + 1)
                    if i == 1:
                        pe.wait_ge(att_ready, b * 4 * H1 + 4 * h + 1)
                    elif h > 0 and i != 0:
                        pe.wait_ge(att_ready, b * 4 * H1 + 4 * (h - 1) + SCORE_AT[i][2])
                    q = q_r[:, h % 4, P * i:P * i + P]
                    w = P * (i + 1)
                    pe.matmul(score_bank(i), q, k_r[:, h // REP, 0, 0:w], start=True, stop=False)
                    m = pe.matmul(score_bank(i), q, k_r[:, h // REP, 1, 0:w], start=False, stop=True)
                    if i != 2:
                        m.then_inc(s1_psum, 1)

                def turn_p(h, i):
                    if i == TILES[0] and h == 0:
                        pe.wait_ge(k_lo_ready, b * KVH + KVH)
                    if i == TILES[0] and h > 0:
                        pe.wait_ge(pt_a_ready, b * H1 + h)
                        pe.wait_ge(pt_b_ready, b * H1 + h)
                    pe.wait_ge(p_ready, b * 4 * H1 + 4 * h + TILES.index(i) + 1)
                    to = psum[:, 3:6, :].rearrange("p a c -> p (a c)")
                    for j in range(i + 1):
                        at = KEY_AT[j] + P * (i - j)
                        m = pe.transpose(to[:, at:at + P], att[:, h % 3, ROW_AT[i] + P * j:ROW_AT[i] + P * j + P],
                                         ident[:, :])
                    if i == TILES[-1]:
                        m.then_inc(pt_psum, 1)

                def weigh1(p, blocks):
                    if blocks[0] == 0:
                        pe.wait_ge(pt_a_ready, b * H1 + 2 * p + 2)
                        pe.wait_ge(pt_b_ready, b * H1 + 2 * p + 2)
                        if p > 0:
                            pe.wait_ge(o_lo_ready, b * (H1 // 2) + p)
                        else:
                            pe.wait_ge(v1_ready, b * 2 + 2)
                    g = 2 * p // REP
                    for j in blocks:
                        for e in range(2):
                            m = pe.matmul(bank(6)[D1 * e:D1 * e + D1, P * j:T], v1[:, j, D1 * g:D1 * g + D1],
                                          probs_t[:, (2 * p + e) % 4, KEY_AT[j]:KEY_AT[j] + T - P * j],
                                          start=(j == 0), stop=(j == NT - 1))
                    if blocks[-1] == NT - 1:
                        m.then_inc(pv1_done, 1)

                def project(p):
                    pe.wait_ge(o_lo_ready, b * (H1 // 2) + p + 1)
                    product(bank(7), (whi("wo", C * p, C), wlo("wo", C * p, C)), (o_r[:, p % 2, 0, :], o_r[:, p % 2, 1, :]),
                            start=(p == 0), stop=(p == H1 // 2 - 1)).then_inc(wo_psum, 1)

                head("wk", 0, bank(2)).then_inc(k_psum, 1)
                queries(0)
                for g in range(1, KVH):
                    head("wk", g, bank(2 + g)).then_inc(k_psum, 1)
                for t in range(NT):
                    to = bank(6 + t // 2)[:, KVH * D1 * (t % 2):KVH * D1 * (t % 2 + 1)]
                    pe.matmul(to, tok_r[:, P * t:P * t + P], whi("wv", 0, KVH * D1), start=True, stop=False)
                    m = pe.matmul(to, tok_r[:, P * t:P * t + P], wlo("wv", 0, KVH * D1), start=False, stop=True)
                    if t % 2:
                        m.then_inc(v_psum, 1)
                queries(1)
                for s in range(H1 + 5):
                    if s == H1 + 4:
                        start_x(b, 1)
                    for i in (3, 2, 0):
                        if s < H1:
                            scores1(s, i)
                    if 0 <= s - 2 < H1:
                        turn_p(s - 2, TILES[0])
                    if s < H1:
                        scores1(s, TILES[3])
                    if 0 <= s - 2 < H1:
                        for i in TILES[1:]:
                            turn_p(s - 2, i)
                    if s % 2 == 0 and s >= 6:
                        project((s - 6) // 2)
                    if s % 2 == 0 and 0 <= s - 4 < H1:
                        weigh1((s - 4) // 2, (0,))
                    if s % 2 == 1 and 0 <= s - 5 < H1:
                        weigh1((s - 5) // 2, (1, 2, 3))
                    if s % 2 == 1 and s + 3 < H1:
                        queries((s + 3) // 2)
                start_qkv(b, 1)
                pe.wait_ge(wo_copied, b + 1)
                transposes(bank(5), [wo_t[:, P * t:P * t + P] for t in range(NT)]).then_inc(x3_psum, 1)
                pe.wait_ge(xn4_ready, b + 1)
                transposes(bank(6), [xn4[:, t, :] for t in range(NT)]).then_inc(xt4_psum, 1)
                pe.wait_ge(f_lo_ready, b + 1)
                for t in range(NT):
                    ts = slice(P * t, P * t + P)
                    pe.matmul(bank(7)[:, ts], f_r[:, 0, ts], whi("sign", 0, C), start=True, stop=False)
                    m = pe.matmul(bank(7)[:, ts], f_r[:, 1, ts], whi("sign", 0, C), start=False, stop=True)
                m.then_inc(ffn_psum, 1)

            def pe_moe(b):
                pe.wait_ge(xn2_ready, b + 1)
                transposes(bank(0), [xn2[:, t, :] for t in range(NT)]).then_inc(xt2_psum, 1)
                pe.wait_ge(x_tf_ready, b + 1)
                for t in range(NT):
                    m = pe.matmul(bank(1)[:, E * t:E * t + E], x_tf[:, P * t:P * t + P], router_sb[:, :],
                                  start=True, stop=True)
                m.then_inc(score_psum, 1)

                def up(part, e, ft, k, to):
                    at = e * F + P * ft
                    return product(to, (whi(part, at, P), wlo(part, at, P)),
                                   (xg_r[:, k % 2, 0, :], xg_r[:, k % 2, 1, :]))

                def gate_of(k):
                    if k >= 2:
                        pe.wait_ge(gated, b * E + k - 1)
                    pe.matmul(bank(7), pick[:, k - 1:k].broadcast_to([2 * E, P]), g_t[0:2 * E, :],
                              start=True, stop=True).then_inc(gate_psum, 1)

                def down(k):
                    e = order[k]
                    pe.wait_ge(h_lo_dve, b * NE + k + 1)
                    pe.wait_ge(h_lo_pool, b * NE + k + 1)
                    for ft in range(FT):
                        at = (e * FT + ft) * C
                        m = product(bank(6), (whi("wout", at, C), wlo("wout", at, C)),
                                    (h_r[:, k % 2, 0, ft, :], h_r[:, k % 2, 1, ft, :]),
                                    start=(k == 0 and ft == 0), stop=(k == NE - 1 and ft == FT - 1))
                    m.then_inc(expert_psum, 1)

                order = [E] + list(range(E))
                for k, e in enumerate(order):
                    pe.wait_ge(xg_lo_ready, b * NE + k + 1)
                    if k > 0:
                        pe.wait_ge(silu_done, b * NE + k)
                    for ft in range(FT):
                        m = up("win", e, ft, k, bank(2 + ft))
                    m.then_inc(mid_psum, 1)
                    if k == 0:
                        pe.wait_ge(gates_ready, b + 1)
                        transposes(bank(1)[0:2 * E, :], [gates_nat[:, t, :] for t in range(NT)]).then_inc(gt_psum, 1)
                    if k > 0:
                        pe.wait_ge(h_done, b * NE + k)
                    for ft in range(FT):
                        m = up("wsw", e, ft, k, bank(4 + ft))
                    m.then_inc(sw_psum, 1)
                    if k == 0:
                        pe.wait_ge(gt_ready, b + 1)
                        gate_of(1)
                    if k + 2 < NE:
                        gate_of(k + 2)
                    if k > 0:
                        down(k - 1)
                down(NE - 1)
                pe.wait_ge(moe_copied, b + 1)
                transposes(bank(0), [moe_t[:, P * t:P * t + P] for t in range(NT)]).then_inc(moe_psum, 1)
                pe_l1(b)

            pe.wait_ge(ident_ready, 1)
            pe.wait_ge(w_lo_ready, 1)
            start_x(0, 0)
            start_qkv(0, 0)
            with pe.Fori(0, NB) as b:
                def turn_k(g):
                    transposes(bank(g), [nat_k[:, t, G0 * g:G0 * g + G0, :] for t in range(NT)]).then_inc(kt_psum, 1)

                def turn_q0(g):
                    transposes(bank(4 + g), [nat_q[:, t, G0 * g:G0 * g + G0, :] for t in range(NT)]).then_inc(qt_psum, 1)

                pe.wait_ge(pads_ready, b + 1)
                pe.wait_ge(k_hi_twice, b + 1)
                pe.wait_ge(k_lo_in, b + 1)
                turn_k(0)
                turn_k(1)
                pe.wait_ge(q_lo_in, b + 1)
                turn_q0(0)
                turn_q0(1)
                turn_q0(2)
                turn_k(2)
                turn_q0(3)
                turn_k(3)

                def scores(h, tiles):
                    g = h // G0
                    for i in tiles:
                        n = h * NT + i
                        if n == 2:
                            pe.wait_ge(qt_ready, b * (NG - 1) + 2)
                        if n >= 3:
                            pe.wait_ge(max_done, b * 64 + n - (2 if n <= G0 * NT else 1))
                        if g == 0:
                            rows = slice(ROWS * h, ROWS * h + ROWS)
                            left, right = q_t[rows, 0, P * i:P * i + P], k_t[rows, 0, :]
                        else:
                            if i == 0:
                                pe.wait_ge(qz_ready[h % G0], b * 16 * (NG - 1) + 16 * g)
                            left, right = q_z[:, h % G0, P * i:P * i + P], k_t[:, g, :]
                        pe.matmul(max_bank(n), left, right, start=True, stop=True).then_inc(s_psum, 1)

                def scores_t(q, half):
                    g, kb = q // NT, q % NT
                    n = 2 * q + half
                    if n >= 2:
                        pe.wait_ge(exp_done, b * 32 + n - 1)
                    if n % (2 * NT) == 0:
                        pe.wait_ge(kz_ready[g % 2], (b * (NG // 2) + g // 2 + 1) * 16 * G0)
                    for j in range(2 * half, 2 * half + 2):
                        m = pe.matmul(bank(j), k_z[:, g % 2, j, P * kb:P * kb + P], q_t[:, g, :],
                                      start=True, stop=True)
                    m.then_inc(st_psum, 1)

                def weigh(q):
                    g, kb = q // NT, q % NT
                    pe.wait_ge(exp_done, b * 32 + 2 * q + 2)
                    if kb == 0 and g > 0:
                        pe.wait_ge(o_copied, b * NG + g)
                    if q == 0:
                        pe.wait_ge(v_ready, b + 1)
                    for j in range(G0):
                        r = ROWS * j
                        at = VW * (G0 * g + j)
                        m = pe.matmul(bank(6)[r:r + ROWS, :], v_nat[:, kb, at:at + ROWS], probs[:, q % 2, j, :],
                                      start=(kb == 0), stop=(kb == NT - 1))
                    m.then_inc(pv_done, 1)

                def turn_q(g):
                    pe.wait_ge(max_in_q, b * NG + g + 1)
                    if g >= 2:
                        pe.wait_ge(on_ready, b * NG + g - 1)
                    elif g == 1:
                        pe.wait_ge(qm_ready, b * NG + 1)
                    transposes(bank(7), [nat_q[:, t, G0 * g:G0 * g + G0, :] for t in range(NT)]).then_inc(qm_psum, 1)

                def turn_o(g):
                    pe.wait_ge(o_copied, b * NG + g + 1)
                    if g > 0:
                        pe.wait_ge(on_ready, b * NG + g)
                    pe.wait_ge(qm_ready, b * NG + min(g + 2, NG))
                    transposes(bank(7), [o_t[:, P * t:P * t + P] for t in range(NT)]).then_inc(on_psum, 1)

                pe.wait_ge(qt_first, b + 1)
                pe.wait_ge(kt_ready, b * NG + 1)
                pe.wait_ge(qt_ready, b * (NG - 1) + 1)
                for h in range(G0):
                    scores(h, range(NT))
                pe.wait_ge(kt_ready, b * NG + NG)
                pe.wait_ge(qt_ready, b * (NG - 1) + NG - 1)
                scores(G0, (0, 1))
                turn_q(0)
                scores(G0, (2, 3))
                pe.wait_ge(qm_ready, b * NG + 1)
                for q in range(H0):
                    g, kb = q // NT, q % NT
                    h = q + LEAD
                    if h < H0:
                        scores(h, (0, 1))
                    if kb == 0 and g > 0:
                        pe.wait_ge(qm_ready, b * NG + g + 1)
                    scores_t(q, 0)
                    if h < H0:
                        scores(h, (2,))
                    if kb == NT - 1 and g + 1 < NG:
                        turn_q(g + 1)
                    scores_t(q, 1)
                    if h < H0:
                        scores(h, (3,))
                    if q > 0:
                        weigh(q - 1)
                    if kb == 1 and g > 0:
                        turn_o(g - 1)
                weigh(H0 - 1)
                turn_o(NG - 1)
                pe.wait_ge(on_ready, b * NG + NG)
                transposes(bank(0), [o_nat[:, t, :] for t in range(NT)]).then_inc(ot_psum, 1)
                pe.wait_ge(ot_lo_ready, b + 1)
                for t in range(NT):
                    ts = slice(P * t, P * t + P)
                    m = product(bank(1)[:, ts], (a_t[:, 0, ts], a_t[:, 1, ts]), (whi("proj", 0, C), wlo("proj", 0, C)))
                m.then_inc(proj_psum, 1)
                pe_moe(b)


def layout(g):
    import numpy as np
    w = np.zeros((P, NW), np.float32)

    def put(part, a):
        w[:, COL[part]:COL[part] + a.shape[1]] = a

    put("qkv", g["L0_attn_w_qkv"].T)
    put("proj", g["L0_attn_w_proj"].T)
    for e in range(E):
        w[:, COL["win"] + F * e:COL["win"] + F * (e + 1)] = g["L0_ffn_w_in_eDF"][e]
        w[:, COL["wsw"] + F * e:COL["wsw"] + F * (e + 1)] = g["L0_ffn_w_swiglu_eDF"][e]
    w[:, COL["win"] + F * E:COL["win"] + F * NE] = g["L0_ffn_w_in_shared_FD"].T
    w[:, COL["wsw"] + F * E:COL["wsw"] + F * NE] = g["L0_ffn_w_swiglu_FD"].T
    wout = np.concatenate([g["L0_ffn_w_out_eFD"], g["L0_ffn_w_out_shared_DF"].T[None]], 0)
    put("wout", wout.reshape(NE, FT, P, C).transpose(2, 0, 1, 3).reshape(P, NE * FT * C))
    ins = {"x": g["L0_attn_x"], "w_all": w, "b_qkv": g["L0_attn_b_qkv"], "b_proj": g["L0_attn_b_proj"],
           "qn_w": g["L0_attn_qn_w"], "kn_w": g["L0_attn_kn_w"], "router": g["L0_ffn_router_DE"],
           "angle": g["L1_attn_q_phase_angle"], "slopes": g["L1_attn_alibi_log_slopes"]}
    twice = lambda a: np.concatenate([a, a], 0)
    put("wq", twice(g["L1_attn_Wq"]))
    put("wk", twice(np.repeat(g["L1_attn_Wk"].reshape(-1, KVH, 1, D1), 2, 2).reshape(-1, 2 * KVH * D1)))
    put("wv", twice(g["L1_attn_Wv"]))
    put("wo", g["L1_attn_Wo"].reshape(H1 * D1 // P, P, C).transpose(1, 0, 2).reshape(P, -1))
    put("sign", g["L1_ffn_weight"].T)
    return ins


def kernel(**inputs):
    import numpy as np
    import concourse.bacc as bacc
    from concourse.bass_utils import run_bass_kernel_spmd

    arrays = layout({name: np.asarray(a) for name, a in inputs.items()})
    nc = bacc.Bacc("TRN2", target_bir_lowering=False, num_devices=1)
    aps = {name: nc.dram_tensor(f"in_{name}", a.shape, mybir.dt.from_np(a.dtype), kind="ExternalInput").ap()
           for name, a in arrays.items()}
    out = nc.dram_tensor("out", arrays["x"].shape, F32, kind="ExternalOutput").ap()
    kernel_program(nc, out=out, **aps)
    result = run_bass_kernel_spmd(nc, [{f"in_{name}": a for name, a in arrays.items()}], core_ids=[0])
    return result.results[0]["out"]
```
